# Optimizing a Trainium2 kernel written in Bass

```python
import numpy as np
import jax
import jax.numpy as jnp

def _softmax(x, axis=-1):
    return jax.nn.softmax(x, axis=axis)

def _gelu(x):
    return jax.nn.gelu(x, approximate=True)

def _silu(x):
    return jax.nn.silu(x)

def _sigmoid(x):
    return jax.nn.sigmoid(x)

def _layernorm(x, axis=-1, eps=1e-05):
    m = jnp.mean(x, axis=axis, keepdims=True)
    v = jnp.var(x, axis=axis, keepdims=True)
    return (x - m) / jnp.sqrt(v + eps)

def _scatter_add(tgt, idx, src, axis=0):
    return tgt.at[idx].add(src)

def _segment_sum(src, seg, n):
    return jax.ops.segment_sum(src, seg, n)
kernel_name = 'mk_gnn_resnorm_d1_gnn_r64_184bc8'

def setup_inputs(seed: int=0):
    np.random.seed(seed)
    _w = jnp.asarray

    def _rec_inputs():
        import jax
        import jax.numpy as jnp
        _gk = jax.random.key(seed)
        x = -0.0003713 + 1 * jax.random.normal(jax.random.fold_in(_gk, 1), (50000, 256), jnp.float32)
        src = jax.random.randint(jax.random.fold_in(_gk, 2), (25000,), 0, 50000, jnp.int32)
        dst = jnp.minimum((50000 * jax.random.uniform(jax.random.fold_in(_gk, 3), (25000,)) ** 2.0).astype(jnp.int32), 49999)
        _o = jnp.argsort(dst, stable=True)
        src = src[_o]
        dst = dst[_o]
        return (x, src, dst)
    x, src, dst = _rec_inputs()

    def _L0_gnn_setup():
        import jax, jax.numpy as jnp
        import numpy as np
        N = 50000
        E = 500000
        D = 256
        key = jax.random.key(seed)
        ks = jax.random.split(key, 12)
        s = 0.02
        x = jax.random.normal(ks[0], (N, D), dtype=jnp.float32)
        edge_index = jax.random.randint(ks[1], (2, E), 0, N, dtype=jnp.int64)
        W1 = jax.random.normal(ks[2], (D, 2 * D), dtype=jnp.float32) * s
        b1 = jax.random.normal(ks[3], (D,), dtype=jnp.float32) * s
        W2 = jax.random.normal(ks[4], (D, D), dtype=jnp.float32) * s
        b2 = jax.random.normal(ks[5], (D,), dtype=jnp.float32) * s
        w_ih = jax.random.normal(ks[6], (3 * D, D), dtype=jnp.float32) * s
        w_hh = jax.random.normal(ks[7], (3 * D, D), dtype=jnp.float32) * s
        b_ih = jax.random.normal(ks[8], (3 * D,), dtype=jnp.float32) * s
        b_hh = jax.random.normal(ks[9], (3 * D,), dtype=jnp.float32) * s
        gamma = jnp.ones((D,), dtype=jnp.float32)
        beta = jnp.zeros((D,), dtype=jnp.float32)
        return {'x': x, 'edge_index': edge_index, 'W1': W1, 'b1': b1, 'W2': W2, 'b2': b2, 'w_ih': w_ih, 'w_hh': w_hh, 'b_ih': b_ih, 'b_hh': b_hh, 'gamma': gamma, 'beta': beta}
    _L0_gnn_all = _L0_gnn_setup()
    _L0_gnn_in = {k: v for k, v in _L0_gnn_all.items() if k in ('W1', 'b1', 'W2', 'b2', 'w_ih', 'w_hh', 'b_ih', 'b_hh', 'gamma', 'beta')}
    del _L0_gnn_all
    return {'x': x, 'src': src, 'dst': dst, 'L0_gnn_W1': _L0_gnn_in['W1'], 'L0_gnn_b1': _L0_gnn_in['b1'], 'L0_gnn_W2': _L0_gnn_in['W2'], 'L0_gnn_b2': _L0_gnn_in['b2'], 'L0_gnn_w_ih': _L0_gnn_in['w_ih'], 'L0_gnn_w_hh': _L0_gnn_in['w_hh'], 'L0_gnn_b_ih': _L0_gnn_in['b_ih'], 'L0_gnn_b_hh': _L0_gnn_in['b_hh'], 'L0_gnn_gamma': _L0_gnn_in['gamma'], 'L0_gnn_beta': _L0_gnn_in['beta']}

def reference(x, src, dst, L0_gnn_W1, L0_gnn_b1, L0_gnn_W2, L0_gnn_b2, L0_gnn_w_ih, L0_gnn_w_hh, L0_gnn_b_ih, L0_gnn_b_hh, L0_gnn_gamma, L0_gnn_beta):
    import jax
    import jax.numpy as jnp

    def _L0_gnn_ref(x, edge_index, W1, b1, W2, b2, w_ih, w_hh, b_ih, b_hh, gamma, beta):
        import jax, jax.numpy as jnp
        import numpy as np
        N = 50000
        E = 500000
        D = 256
        n_nodes = x.shape[0]
        row, col = (edge_index[0], edge_index[1])
        h = jnp.concatenate([x[row], x[col]], axis=-1)
        msgs = jax.nn.silu(h @ W1.T + b1) @ W2.T + b2
        agg = jax.ops.segment_sum(msgs, row, num_segments=n_nodes)
        cnt = jax.ops.segment_sum(jnp.ones((row.shape[0], 1), x.dtype), row, num_segments=n_nodes)
        agg = agg / (cnt + 1e-08)
        gi = agg @ w_ih.T + b_ih
        gh = x @ w_hh.T + b_hh
        i_r, i_z, i_n = jnp.split(gi, 3, axis=-1)
        h_r, h_z, h_n = jnp.split(gh, 3, axis=-1)
        r = jax.nn.sigmoid(i_r + h_r)
        z = jax.nn.sigmoid(i_z + h_z)
        n = jnp.tanh(i_n + r * h_n)
        x_new = (1.0 - z) * n + z * x
        mu = jnp.mean(x_new, axis=-1, keepdims=True)
        var = jnp.var(x_new, axis=-1, keepdims=True)
        return gamma * (x_new - mu) / jnp.sqrt(var + 1e-05) + beta
    edge_index = jnp.stack([src, dst])
    x = _layernorm(x + _L0_gnn_ref(x, edge_index, L0_gnn_W1, L0_gnn_b1, L0_gnn_W2, L0_gnn_b2, L0_gnn_w_ih, L0_gnn_w_hh, L0_gnn_b_ih, L0_gnn_b_hh, L0_gnn_gamma, L0_gnn_beta), axis=-1)
    return x

_drawn_inputs = setup_inputs


def setup_inputs(seed=0):
    import zlib

    import numpy as np

    out = dict(_drawn_inputs(seed))
    spreads = {'L0_gnn_gamma': (1.0, 0.2), 'L0_gnn_beta': (0.0, 0.1)}
    factors = {'L0_gnn_W1': 7.12,
     'L0_gnn_b1': 8.0,
     'L0_gnn_W2': 6.92,
     'L0_gnn_b2': 8.0,
     'L0_gnn_w_ih': 6.696,
     'L0_gnn_b_ih': 5.35,
     'L0_gnn_b_hh': 8.0}
    for name, (base, spread) in spreads.items():
        noise = np.random.default_rng([zlib.crc32(name.encode()), seed]).standard_normal(out[name].shape)
        drawn = base * np.exp(spread * noise) if base else spread * noise
        out[name] = jnp.asarray(drawn.astype(out[name].dtype))
    for name, factor in factors.items():
        out[name] = (out[name] * factor).astype(out[name].dtype)
    return out
```

```python
from contextlib import ExitStack

import numpy as np

import concourse.bass as bass
from concourse import mybir

P = 128
D = 256
KC = D // P
NODES = 50000
EDGES = 25000
BLOCKS = 392
NODES_PAD = BLOCKS * P
TILES = 196
EDGES_PAD = TILES * P
EU = 4
NU = 8
CNT = D
LOC = D + 2
SUMMED = D + 2
HALF = D + 4
ROW = 2 * HALF
EMPTY = float(1 << 20)
EPS_LN = 1e-5
EPS_CNT = 1e-8

C_IDENT, C_LOWER, C_UPTO, C_IOTA = 0, P, 2 * P, 3 * P
C_BLOCK = 4 * P
C_TILE = C_BLOCK + BLOCKS
C_PART = C_TILE + TILES
C_LO1 = C_PART + 1
C_LO4 = C_LO1 + 1
C_SEL4 = C_LO4 + 1
C_HALF = C_SEL4 + 4
C_ALL = C_HALF + 1


def constants():
    c = np.zeros((P, C_ALL), np.float32)
    i = np.arange(P)
    c[:, C_IDENT:C_IDENT + P] = np.eye(P)
    c[:, C_LOWER:C_LOWER + P] = i[:, None] < i[None, :]
    c[:, C_UPTO:C_UPTO + P] = i[:, None] >= i[None, :]
    c[:, C_IOTA:C_IOTA + P] = i[None, :]
    c[:, C_BLOCK:C_BLOCK + BLOCKS] = np.arange(BLOCKS)[None, :]
    c[:, C_TILE:C_TILE + TILES] = np.arange(TILES)[None, :]
    c[:, C_PART] = i + 1
    c[:, C_LO1] = np.where(i == 1, -1, 0)
    c[:, C_LO4] = np.where(i % 2 == 1, -1, 0)
    c[:, C_SEL4:C_SEL4 + 4] = np.array([0, 0, 1, 1])[None, :]
    c[:, C_HALF] = -0.5
    return c


def gnn_layer(nc, x, src, dst, w1t, b1, w2, b2, wiht, whht, bih, bhh, gamma, beta, consts, out):
    f32, f32r, bf16, i32 = mybir.dt.float32, mybir.dt.float32r, mybir.dt.bfloat16, mybir.dt.int32
    fp16 = mybir.dt.float16
    ACT, ALU = mybir.ActivationFunctionType, mybir.AluOpType
    ctx = ExitStack()
    with ctx:
        def sb(name, shape, dt=f32):
            return ctx.enter_context(nc.sbuf_tensor(name, shape, dt))

        def sem(name):
            return ctx.enter_context(nc.semaphore(name))

        def sems(name, n):
            return [sem(f"{name}{i}") for i in range(n)]

        messages = nc.dram_tensor("messages", [EDGES_PAD, ROW], f32, kind="Internal").ap()
        sums = nc.dram_tensor("sums", [NODES_PAD, ROW], f32, kind="Internal").ap()

        cst = sb("cst", [P, C_ALL])
        ident = cst[:, C_IDENT:C_IDENT + P]
        lower = sb("lower", [P, P], bf16)
        upto = sb("upto", [P, P], bf16)
        iota = sb("iota", [P, P], fp16)
        blocks = sb("blocks", [P, BLOCKS], fp16)
        iota1 = sb("iota1", [P, P])
        srci = sb("srci", [P, TILES], i32)
        dsti = sb("dsti", [P, TILES], i32)
        blki = sb("blki", [P, TILES], i32)
        loci = sb("loci", [P, TILES], i32)
        blkf = sb("blkf", [P, TILES])
        locf = sb("locf", [P, TILES])
        ranks = sb("ranks", [P, TILES])
        slot_row = sb("slot_row", [P, BLOCKS], i32)
        slot_used = sb("slot_used", [P, BLOCKS])
        slot_a = sb("slot_a", [P, BLOCKS])
        slot_b = sb("slot_b", [P, BLOCKS])
        w1h, w1l = sb("w1h", [P, 2 * KC, D], f32r), sb("w1l", [P, 2 * KC, D], f32r)
        wxh, wxl = sb("wxh", [P, KC, 3 * D], f32r), sb("wxl", [P, KC, 3 * D], f32r)
        wsh, wsl = sb("wsh", [P, KC, 3 * D], f32r), sb("wsl", [P, KC, 3 * D], f32r)
        stage = sb("stage", [P, 2 * KC * D])
        wih = sb("wih", [P, KC, 3 * D])
        whh = sb("whh", [P, KC, 3 * D])
        w2s = sb("w2s", [P, KC, D])
        b2s = sb("b2s", [P, KC, 4])
        brow = sb("brow", [1, 3 * D + 3 * D + D])
        bias = sb("bias", [4, 4 * D], f32r)
        biash = sb("biash", [4, 4 * D], f32r)
        bias1 = sb("bias1", [2, D], f32r)
        bias1h = sb("bias1h", [2, D], f32r)
        ones = sb("ones", [2, P], f32r)
        gammab, betab = sb("gammab", [P, D]), sb("betab", [P, D])

        XE = 4
        src_now, dst_now = sb("src_now", [P, 2, EU], i32), sb("dst_now", [P, 2, EU], i32)
        rows_now = sb("rows_now", [P, NU], i32)
        xsrc, xdst = sb("xsrc", [P, XE, D]), sb("xdst", [P, XE, D])
        eh, el = sb("eh", [P, 2, 2 * KC * P], f32r), sb("el", [P, 2, 2 * KC * P], f32r)
        sil = sb("sil", [P, 2, D])
        msg = sb("msg", [P, EU, ROW], f32r)
        ohb = sb("ohb", [P, 2, BLOCKS], bf16)
        picked = sb("picked", [P, BLOCKS], bf16)
        rank = sb("rank", [P, 2])
        oha, oht = sb("oha", [P, 2, P], bf16), sb("oht", [P, 2, P], bf16)

        xs = sb("xs", [P, NU, D])
        mg = sb("mg", [P, 4, ROW], f32r)
        oh = sb("oh", [P, 4, P], f32r)
        xh, xl = sb("xh", [P, 4, D], f32r), sb("xl", [P, 4, D], f32r)
        mean = sb("mean", [P, 2, HALF])
        sh, sl = sb("sh", [P, 2, D], f32r), sb("sl", [P, 2, D], f32r)
        hasrow = sb("hasrow", [4, 2, P], f32r)
        cnt_eps, rcount = sb("cnt_eps", [P, 4]), sb("rcount", [P, 4])
        rz = sb("rz", [P, 4, 2 * D])
        rhn, npre, nt = sb("rhn", [P, 2, D]), sb("npre", [P, 2, D]), sb("nt", [P, 4, D])
        diff, xb = sb("diff", [P, 4, D]), sb("xb", [P, 4, D])
        zd, xn = sb("zd", [P, 2, D]), sb("xn", [P, 2, D])
        st1, ag1, rs1 = sb("st1", [P, 4, 6]), sb("ag1", [P, 4, 2]), sb("rs1", [P, 4])
        st2, ag2, rs2 = sb("st2", [P, 4, 6]), sb("ag2", [P, 4, 2]), sb("rs2", [P, 4])
        ve1, ve2, nmr = sb("ve1", [P, 4]), sb("ve2", [P, 4]), sb("nmr", [P, 4])
        tg, uu, yy = sb("tg", [P, 2, D]), sb("uu", [P, 4, D]), sb("yy", [P, 4, D])

        top, levf, levi = sb("top", [P, 1]), sb("levf", [1, 1]), sb("levi", [1, 1], i32)
        levels = sb("levels", [1, 1], i32)
        before, total, put = sb("before", [P, ROW], f32r), sb("total", [P, 2, SUMMED]), sb("put", [P, ROW], f32r)

        banks = [ctx.enter_context(nc.psum_tensor(f"bank{i}", [P, 512], f32)) for i in range(8)]
        pe_t, pe_m = banks[0:2], banks[2:4]
        p_cum, p_sa, p_sb = banks[4], banks[5], banks[6]
        pn_t, pn_s, pn_rz, pn_n = banks[0:2], banks[2:4], banks[4:6], banks[6:8]

        ld_w = sem("ld_w")
        ld_e = sem("ld_e")
        cst_ready, w_split, setup_mm, setup_cp, idx_ready = (
            sem("cst_ready"), sem("w_split"), sem("setup_mm"), sem("setup_cp"), sem("idx_ready"))
        w_step = sem("w_step")
        got_src, got_dst, e_stored = sems("got_src", XE), sems("got_dst", XE), sems("e_stored", EU)
        e_xt, e_hi, e_lo, e_mm, e_msg, e_loc = (sem(n) for n in ("e_xt", "e_hi", "e_lo", "e_mm", "e_msg", "e_loc"))
        e_mh, e_ml = sem("e_mh"), sem("e_ml")
        e_oh, e_cum, e_rank, e_one, e_tab = (sem(n) for n in ("e_oh", "e_cum", "e_rank", "e_one", "e_tab"))
        idx_now = sem("idx_now")
        pool_passed, dve_passed, sp_passed = sem("pool_passed"), sem("dve_passed"), sem("sp_passed")
        t_step, tab_ready = sem("t_step"), sem("tab_ready")
        lv_top, lv_row, lv_ready = sem("lv_top"), sem("lv_row"), sem("lv_ready")
        v_zero, v_oh, v_tab, v_step, v_rows = (sem(n) for n in ("v_zero", "v_oh", "v_tab", "v_step", "v_rows"))
        v_idx, v_got, v_one, v_sum, v_prev = (sem(n) for n in ("v_idx", "v_got", "v_one", "v_sum", "v_prev"))
        v_acc, v_add, v_put, v_done = (sem(n) for n in ("v_acc", "v_add", "v_put", "v_done"))
        got_x, got_m, n_stored = sems("got_x", NU), sems("got_m", 4), sems("n_stored", 4)
        names = ("n_oh n_xt n_xh n_xl n_seg n_ce n_rc n_mean n_st n_sh n_has n_sl n_mm n_rz n_rhn n_npre n_tanh"
                 " n_diff n_xb n_zd n_xn n_s1 n_a1 n_v1 n_r1 n_tg n_u n_s2 n_a2 n_v2 n_r2 n_nmr n_y").split()
        S = {n: sem(n) for n in names}

        def need(eng, s, value):
            if not isinstance(value, int) or value > 0:
                eng.wait_ge(s, value)

        def need_apart(eng, passed, s, value):
            need(eng, s, value)
            eng.sem_inc(passed)

        def uses(j, slots, u):
            return j // slots if isinstance(j, int) else (j - u) // slots

        block = ctx.enter_context(nc.Block())
        W_LOADS = 14

        @block.sync
        def _(sp):
            loads = [(cst[:, :], consts), (srci[:, :], src.rearrange("(p t) -> p t", p=P)),
                     (dsti[:, :], dst.rearrange("(p t) -> p t", p=P))]
            for a, b in loads:
                sp.dma_start(a, b).then_inc(ld_e, 16)
            more = [(stage[:, :].rearrange("p (k n) -> p k n", n=D), w1t.rearrange("(k p) n -> p k n", p=P)),
                    (wih[:, :, :], wiht.rearrange("(k p) n -> p k n", p=P)),
                    (w2s[:, :, :], w2.rearrange("(k p) n -> p k n", p=P)),
                    (whh[:, :, :], whht.rearrange("(k p) n -> p k n", p=P)),
                    (brow[:, 0:3 * D], bih.rearrange("(a n) -> a n", a=1)),
                    (brow[:, 3 * D:6 * D], bhh.rearrange("(a n) -> a n", a=1)),
                    (brow[:, 6 * D:7 * D], b1.rearrange("(a n) -> a n", a=1)),
                    (gammab[:, :], gamma.rearrange("(a n) -> a n", a=1).to_broadcast([P, D])),
                    (betab[:, :], beta.rearrange("(a n) -> a n", a=1).to_broadcast([P, D]))]
            for k in range(KC):
                for c in range(2):
                    more.append((b2s[:, k, c:c + 1], b2[k * P:(k + 1) * P].rearrange("(p a) -> p a", a=1)))
            for a, b in more:
                sp.dma_start(a, b).then_inc(ld_w, 16)
            assert len(more) == W_LOADS - 1

            def store_messages(t, u):
                sp.wait_ge(e_ml, t + 1)
                sp.wait_ge(e_loc, t + 1)
                sp.dma_start(messages[bass.ds(t * P, P), :], msg[:, u, :].bitcast(f32)).then_inc(e_stored[u], 16)

            for u in range(EU):
                store_messages(u, u)
            with sp.Fori(1, TILES // EU) as g:
                for u in range(EU):
                    store_messages(g * EU + u, u)

            sp.wait_ge(lv_ready, 1)
            n_levels = sp.value_load(levels[0:1, 0:1], min_val=1, max_val=TILES)
            with sp.If(n_levels > 1):
                sp.wait_ge(v_zero, 2)
                with sp.Fori(0, BLOCKS) as b:
                    sp.dma_start(sums[bass.ds(b * P, P), :], put[:, :].bitcast(f32)).then_inc(v_put, 16)
                    need_apart(sp, sp_passed, v_put, b * 16 + 16)
                with sp.Fori(0, n_levels) as lv:
                    with sp.Fori(0, BLOCKS) as b:
                        n = lv * BLOCKS + b
                        sp.dma_start(before[:, :].bitcast(f32), sums[bass.ds(b * P, P), :]).then_inc(v_prev, 16)
                        need_apart(sp, sp_passed, v_add, n + 1)
                        sp.dma_start(sums[bass.ds(b * P, P), :], put[:, :].bitcast(f32)).then_inc(v_put, 16)
                        need_apart(sp, sp_passed, v_put, n * 16 + 16 * (BLOCKS + 1))
                sp.sem_inc(v_done)

            def load_x(j, u):
                need(sp, S["n_diff"], j - NU + 1)
                need(sp, S["n_xb"], j - NU + 1)
                need(sp, S["n_xt"], j - NU + 1)
                sp.dma_start(xs[:, u, :], x[bass.ds(j * P, P), :]).then_inc(got_x[u], 16)

            def store_y(j, u):
                sp.wait_ge(S["n_y"], j + 1)
                sp.dma_start(out[bass.ds(j * P, P), :], yy[:, u % 4, :]).then_inc(n_stored[u % 4], 16)

            AHEAD, BEHIND = 5, 5

            def turn(i, first=0):
                for u in range(NU):
                    b = i + u
                    front, back = b + AHEAD, b - BEHIND
                    if not isinstance(i, int) or front < BLOCKS:
                        load_x(front, (u + AHEAD) % NU)
                    if not isinstance(i, int) or back >= 0:
                        store_y(back, (u - BEHIND) % NU)

            for j in range(AHEAD):
                load_x(j, j)
            turn(0)
            with sp.Fori(1, BLOCKS // NU - 1) as g:
                turn(g * NU)
            turn(BLOCKS - NU)
            for j in range(BLOCKS - BEHIND, BLOCKS):
                store_y(j, j % NU)
            for s in range(4):
                sp.wait_ge(n_stored[s], 16 * (BLOCKS // 4))

        def gather(dst_tile, table, rows, done, bound=None):
            nc.gpsimd.indirect_dma_start(
                out=dst_tile, out_offset=None, in_=rows,
                in_offset=bass.IndirectOffsetOnAxis(ap=table, axis=0),
                bounds_check=bound, oob_is_err=False).then_inc(done, 16)

        @block.gpsimd
        def _(pool):
            last_row = pool.to_reg(EDGES_PAD - 1)
            nc.gpsimd.memset(msg[:, :, 0:HALF].bitcast(f32), 1.0).then_inc(cst_ready, 1)
            nc.gpsimd.memset(msg[:, :, HALF:ROW].bitcast(f32), 0.0).then_inc(cst_ready, 1)
            nc.gpsimd.memset(mg[:, :, :].bitcast(f32), 0.0).then_inc(cst_ready, 1)
            nc.gpsimd.memset(mean[:, :, :], 1.0).then_inc(cst_ready, 1)
            pool.wait_ge(ld_e, 48)

            def gather_edges(t0, turn_no, side):
                if not isinstance(turn_no, int) or turn_no >= 2:
                    for u in range(EU):
                        pool.wait_ge(got_dst[u], 16 * (turn_no - 1))
                nc.gpsimd.tensor_copy(src_now[:, side, :], srci[:, bass.ds(t0, EU)]).then_inc(idx_now, 1)
                nc.gpsimd.tensor_copy(dst_now[:, side, :], dsti[:, bass.ds(t0, EU)]).then_inc(idx_now, 1)
                pool.wait_ge(idx_now, 2 * turn_no + 2)
                for u in range(EU):
                    need_apart(pool, pool_passed, e_xt, t0 + (u - XE + 1))
                    gather(xsrc[:, u, :], src_now[:, side, u:u + 1], x, got_src[u])
                    gather(xdst[:, u, :], dst_now[:, side, u:u + 1], x, got_dst[u])

            E_TURNS = TILES // EU
            gather_edges(0, 0, 0)
            with pool.Fori(0, E_TURNS // 2) as g:
                for side in range(2):
                    gather_edges((g * 2 + (side + 1)) * EU, g * 2 + (side + 1), (side + 1) % 2)

            for u in range(EU):
                pool.wait_ge(e_stored[u], 16 * (TILES // EU))
            pool.wait_ge(tab_ready, 1)
            def node_stage(summed):
                AHEAD = NU // 2

                def gather_rows(j, u):
                    need_apart(pool, pool_passed, S["n_seg"], j - 3)
                    if summed:
                        nc.gpsimd.dma_start(mg[:, u % 4, :].bitcast(f32), sums[bass.ds(j * P, P), :]).then_inc(got_m[u % 4], 16)
                    else:
                        gather(mg[:, u % 4, :].bitcast(f32), rows_now[:, u:u + 1], messages, got_m[u % 4], last_row)

                def add_beta(j, u):
                    need(pool, S["n_u"], j - 3)
                    pool.wait_ge(got_x[u], 16 * (uses(j, NU, u) + 1))
                    nc.gpsimd.tensor_tensor(out=xb[:, u % 4, :], in0=xs[:, u, :], in1=betab[:, :], op=ALU.add)\
                        .then_inc(S["n_xb"], 1)

                def subtract_n(j, u):
                    need(pool, S["n_zd"], j - 3)
                    pool.wait_ge(S["n_tanh"], j + 1)
                    nc.gpsimd.tensor_tensor(out=diff[:, u % 4, :], in0=xs[:, u, :], in1=nt[:, u % 4, :],
                                            op=ALU.subtract).then_inc(S["n_diff"], 1)

                def inv_std(j, u, before, ve, free, rs, done):
                    pool.wait_ge(before, j + 1)
                    need(pool, free, j - 3)
                    nc.gpsimd.tensor_tensor(out=rs[:, u % 4:u % 4 + 1], in0=ve[:, u % 4:u % 4 + 1],
                                            in1=cst[:, C_HALF:C_HALF + 1], op=ALU.pow).then_inc(done, 1)

                def inv_std1(j, u):
                    inv_std(j, u, S["n_v1"], ve1, S["n_u"], rs1, S["n_r1"])

                def inv_std2(j, u):
                    inv_std(j, u, S["n_v2"], ve2, S["n_y"], rs2, S["n_r2"])

                def copy_rows(j0, u0, half_no):
                    need(pool, S["n_oh"], j0 - NU + NU // 2)
                    nc.gpsimd.tensor_copy(rows_now[:, u0:u0 + NU // 2], slot_row[:, bass.ds(j0, NU // 2)])\
                        .then_inc(idx_now, 1)
                    pool.wait_ge(idx_now, 2 * E_TURNS + 1 + half_no)

                def turn(i, turn_no):
                    for u in range(NU):
                        b = i + u
                        fixed = isinstance(i, int)
                        if not fixed or 0 <= b + AHEAD < BLOCKS:
                            if u % AHEAD == 0 and not summed:
                                copy_rows(b + AHEAD, (u + AHEAD) % NU, turn_no * 2 + (1 + u // AHEAD))
                            gather_rows(b + AHEAD, (u + AHEAD) % NU)
                        for part, lag in ((inv_std1, -3), (inv_std2, -4), (add_beta, -1), (subtract_n, -1)):
                            if not fixed or 0 <= b + lag < BLOCKS:
                                part(b + lag, (u + lag) % NU)

                if not summed:
                    copy_rows(0, 0, 0)
                for j in range(AHEAD):
                    gather_rows(j, j)
                turn(0, 0)
                with pool.Fori(1, BLOCKS // NU - 1) as g:
                    turn(g * NU, g)
                turn(BLOCKS - NU, BLOCKS // NU - 1)
                turn(BLOCKS, BLOCKS // NU)

            pool.wait_ge(ld_w, 16 * (W_LOADS - 1))
            pool.wait_ge(lv_ready, 1)
            n_levels = pool.value_load(levels[0:1, 0:1], min_val=1, max_val=TILES)
            with pool.If(n_levels > 1):
                with pool.Fori(0, n_levels) as lv:
                    with pool.Fori(0, BLOCKS) as b:
                        n = lv * BLOCKS + b
                        pool.wait_ge(v_rows, lv + 1)
                        pool.wait_ge(v_sum, n + 1)
                        nc.gpsimd.tensor_copy(rows_now[:, 0:1], slot_row[:, bass.ds(b, 1)]).then_inc(v_idx, 1)
                        need_apart(pool, pool_passed, v_idx, n + 1)
                        gather(mg[:, 0, :].bitcast(f32), rows_now[:, 0:1], messages, v_got, last_row)
                pool.wait_ge(v_done, 1)
                pool.wait_ge(tab_ready, 2)
                node_stage(True)
            with pool.Else():
                node_stage(False)

        @block.scalar
        def _(act):
            def edge_hi(t, u):
                act.wait_ge(e_xt, t + 1)
                need(act, e_mm, t - 1)
                nc.scalar.activation(eh[:, u % 2, :], pe_t[u % 2][:, :], ACT.Copy).then_inc(e_hi, 1)

            def edge_silu(t, u):
                act.wait_ge(e_mm, t + 1)
                need(act, e_ml, t - 1)
                nc.scalar.activation(sil[:, u % 2, :], pe_m[u % 2][:, 0:D], ACT.Silu).then_inc(e_msg, 1)

            def edge_message_hi(t, u):
                act.wait_ge(e_msg, t + 1)
                need(act, e_stored[u], 16 * uses(t, EU, u))
                nc.scalar.activation(msg[:, u, 0:D], sil[:, u % 2, :], ACT.Copy).then_inc(e_mh, 1)

            act.wait_ge(cst_ready, 4)
            edge_hi(0, 0)
            for t in range(EU):
                edge_hi(t + 1, (t + 1) % EU)
                edge_silu(t, t)
                edge_message_hi(t, t)
            with act.Fori(1, TILES // EU - 1) as g:
                for u in range(EU):
                    edge_hi(g * EU + (u + 1), (u + 1) % EU)
                    edge_silu(g * EU + u, u)
                    edge_message_hi(g * EU + u, u)
            for t in range(TILES - EU, TILES):
                if t + 1 < TILES:
                    edge_hi(t + 1, (t + 1) % EU)
                edge_silu(t, t % EU)
                edge_message_hi(t, t % EU)

            def gates(j, u):
                act.wait_ge(S["n_mm"], j + 1)
                need(act, S["n_zd"], j - 3)
                nc.scalar.activation(rz[:, u % 4, :], pn_rz[u % 2][:, :], ACT.Sigmoid).then_inc(S["n_rz"], 1)

            def x_hi(j, u):
                act.wait_ge(S["n_xt"], j + 1)
                need(act, S["n_mm"], j - 3)
                nc.scalar.activation(xh[:, u % 4, :], pn_t[u % 2][:, 0:D], ACT.Copy).then_inc(S["n_xh"], 1)

            def mean_rows(j, u):
                act.wait_ge(S["n_rc"], j + 1)
                need(act, S["n_st"], j - 1)
                nc.scalar.activation(mean[:, u % 2, 0:D + 2], pn_s[u % 2][:, 0:D + 2], ACT.Copy,
                                     scale=rcount[:, u % 4:u % 4 + 1]).then_inc(S["n_mean"], 1)

            def s_hi(j, u):
                act.wait_ge(S["n_st"], j + 1)
                need(act, S["n_mm"], j - 1)
                nc.scalar.activation(sh[:, u % 2, :], pn_t[u % 2][:, D:2 * D], ACT.Copy).then_inc(S["n_sh"], 1)
                nc.scalar.activation(hasrow[:, u % 2, :], pn_s[u % 2][0:4, 384:384 + P], ACT.Copy)\
                    .then_inc(S["n_has"], 1)

            def tanh(j, u):
                act.wait_ge(S["n_npre"], j + 1)
                need(act, S["n_xn"], j - 3)
                nc.scalar.activation(nt[:, u % 4, :], npre[:, u % 2, :], ACT.Tanh).then_inc(S["n_tanh"], 1)

            def last_norm(j, u):
                act.wait_ge(S["n_nmr"], j + 1)
                need(act, n_stored[u % 4], 16 * (uses(j, NU, u) * 2 + u // 4))
                nc.scalar.activation(yy[:, u % 4, :], uu[:, u % 4, :], ACT.Identity, bias=nmr[:, u % 4:u % 4 + 1],
                                     scale=rs2[:, u % 4:u % 4 + 1]).then_inc(S["n_y"], 1)

            def turn(i, us=range(NU)):
                for u in us:
                    def on(lag):
                        return not isinstance(i, int) or 0 <= i + u + lag < BLOCKS
                    for part, lag in ((gates, -1), (x_hi, 2), (mean_rows, 2), (s_hi, 1), (tanh, -1), (last_norm, -5)):
                        if on(lag):
                            part(i + u + lag, (u + lag) % NU)

            turn(-NU)
            turn(0)
            with act.Fori(1, BLOCKS // NU - 1) as g:
                turn(g * NU)
            turn(BLOCKS - NU)
            turn(BLOCKS)

        @block.vector
        def _(dve):
            dve.wait_ge(ld_e, 48)
            steps = [
                lambda: nc.vector.tensor_copy(lower[:, :], cst[:, C_LOWER:C_LOWER + P]),
                lambda: nc.vector.tensor_copy(upto[:, :], cst[:, C_UPTO:C_UPTO + P]),
                lambda: nc.vector.tensor_copy(iota[:, :], cst[:, C_IOTA:C_IOTA + P]),
                lambda: nc.vector.tensor_copy(blocks[:, :], cst[:, C_BLOCK:C_BLOCK + BLOCKS]),
                lambda: nc.vector.tensor_scalar(iota1[:, :], cst[:, C_IOTA:C_IOTA + P], 1.0, None, ALU.add),
                lambda: nc.vector.tensor_scalar(blki[:, :], srci[:, :], 7, None, ALU.arith_shift_right),
                lambda: nc.vector.tensor_scalar(loci[:, :], srci[:, :], 127, None, ALU.bitwise_and),
                lambda: nc.vector.tensor_scalar(ones[:, :], cst[0:2, C_IOTA:C_IOTA + P], 0.0, 1.0, ALU.mult, ALU.add),
            ]
            for f in steps:
                f().then_inc(idx_ready, 1)
            dve.wait_ge(idx_ready, len(steps))
            nc.vector.tensor_copy(blkf[:, :], blki[:, :]).then_inc(idx_ready, 1)
            nc.vector.tensor_scalar(locf[:, :], loci[:, :], 1.0, None, ALU.add).then_inc(idx_ready, 1)
            N_IDX = len(steps) + 2
            dve.wait_ge(ld_w, 16 * (W_LOADS - 1))
            w1s = stage[:, :].rearrange("p (k n) -> p k n", n=D)
            nc.vector.tensor_copy(w1h[:, :, :], w1s).then_inc(w_step, 1)
            nc.vector.tensor_copy(wxh[:, :, :], whh[:, :, :]).then_inc(w_step, 1)
            nc.vector.memset(b2s[:, :, 2:4], 0.0).then_inc(w_step, 1)
            dve.wait_ge(w_step, 3)
            nc.vector.tensor_tensor(w1l[:, :, :], w1s, w1h[:, :, :].bitcast(f32), ALU.subtract).then_inc(w_split, 1)
            nc.vector.tensor_tensor(wxl[:, :, :], whh[:, :, :], wxh[:, :, :].bitcast(f32), ALU.subtract)\
                .then_inc(w_split, 1)
            dve.wait_ge(setup_mm, 1)
            nc.vector.tensor_copy(bias1h[:, :], pe_m[0][0:2, 0:D]).then_inc(w_step, 1)
            dve.wait_ge(w_step, 4)
            nc.vector.scalar_tensor_tensor(out=bias1[:, :], in0=bias1h[:, :].bitcast(f32),
                                           scalar=cst[0:2, C_LO1:C_LO1 + 1], in1=pe_m[0][0:2, 0:D],
                                           op0=ALU.mult, op1=ALU.add).then_inc(w_split, 1)
            for k in range(KC):
                dve.wait_ge(setup_mm, 2 + k)
                for c, (bank, n0, n1) in enumerate(((p_sa, 0, 2 * D), (p_sb, 2 * D, 3 * D))):
                    nc.vector.tensor_copy(wsh[:, k, n0:n1], bank[:, 0:n1 - n0]).then_inc(w_step, 1)
                    dve.wait_ge(w_step, 5 + 2 * k + c)
                    nc.vector.tensor_tensor(wsl[:, k, n0:n1], bank[:, 0:n1 - n0], wsh[:, k, n0:n1].bitcast(f32),
                                            ALU.subtract).then_inc(setup_cp, 1)
            dve.wait_ge(setup_mm, 2 + KC)
            for c, (bank, n0) in enumerate(((p_sa, 0), (p_sb, 2 * D))):
                nc.vector.tensor_copy(biash[:, n0:n0 + 2 * D], bank[0:4, :]).then_inc(w_step, 1)
                dve.wait_ge(w_step, 5 + 2 * KC + c)
                nc.vector.scalar_tensor_tensor(out=bias[:, n0:n0 + 2 * D], in0=biash[:, n0:n0 + 2 * D].bitcast(f32),
                                               scalar=cst[0:4, C_LO4:C_LO4 + 1], in1=bank[0:4, :],
                                               op0=ALU.mult, op1=ALU.add).then_inc(setup_cp, 1)

            dve.wait_ge(cst_ready, 4)
            dve.wait_ge(idx_ready, N_IDX)

            def edge_lo(t, u):
                dve.wait_ge(e_hi, t + 1)
                need(dve, e_mm, t - 1)
                nc.vector.tensor_tensor(el[:, u % 2, :], pe_t[u % 2][:, :], eh[:, u % 2, :].bitcast(f32),
                                        ALU.subtract).then_inc(e_lo, 1)

            def edge_block(t, u):
                need(dve, e_tab, t - 1)
                nc.vector.tensor_scalar(ohb[:, u % 2, :], blocks[:, :], blkf[:, bass.ds(t, 1)], None, ALU.is_equal)\
                    .then_inc(e_oh, 1)

            def edge_local(t, u):
                need(dve, e_stored[u], 16 * uses(t, EU, u))
                nc.vector.tensor_copy(msg[:, u, LOC:LOC + 1], locf[:, bass.ds(t, 1)]).then_inc(e_loc, 1)

            def edge_message_lo(t, u):
                dve.wait_ge(e_mh, t + 1)
                nc.vector.tensor_tensor(msg[:, u, HALF:HALF + D], sil[:, u % 2, :], msg[:, u, 0:D].bitcast(f32),
                                        ALU.subtract).then_inc(e_ml, 1)

            def edge_rank(t, u):
                dve.wait_ge(e_cum, t + 1)
                nc.vector.scalar_tensor_tensor(out=picked[:, :], in0=p_cum[:, 0:BLOCKS], scalar=1.0,
                                               in1=ohb[:, u % 2, :], op0=ALU.mult, op1=ALU.mult,
                                               accum_out=rank[:, u % 2:u % 2 + 1]).then_inc(e_rank, 1)

            def edge_slot(t, u):
                dve.wait_ge(e_rank, t + 1)
                need(dve, e_tab, t - 1)
                r = rank[:, u % 2:u % 2 + 1]
                nc.vector.tensor_scalar(oha[:, u % 2, :], iota[:, :], r, cst[:, C_PART:C_PART + 1],
                                        ALU.is_equal, ALU.mult).then_inc(e_one, 1)
                nc.vector.tensor_scalar(oht[:, u % 2, :], iota[:, :], r, cst[:, bass.ds(C_TILE + t, 1)],
                                        ALU.is_equal, ALU.mult).then_inc(e_one, 1)
                nc.vector.tensor_copy(ranks[:, bass.ds(t, 1)], r).then_inc(e_one, 1)

            edge_lo(0, 0)
            edge_block(0, 0)

            def edge_turn(t0, more=True):
                for u in range(EU):
                    t = t0 + u
                    edge_rank(t, u)
                    if not isinstance(t0, int) or t > 0:
                        edge_message_lo(t0 + (u - 1), (u - 1) % EU)
                    if more or u + 1 < EU:
                        edge_block(t0 + (u + 1), (u + 1) % EU)
                    edge_slot(t, u)
                    if more or u + 1 < EU:
                        edge_lo(t0 + (u + 1), (u + 1) % EU)
                    edge_local(t, u)

            edge_turn(0)
            with dve.Fori(1, TILES // EU - 1) as g:
                edge_turn(g * EU)
            edge_turn(TILES - EU, more=False)
            edge_message_lo(TILES - 1, (TILES - 1) % EU)

            dve.wait_ge(e_tab, TILES)
            def make_table(step, n, done):
                nc.vector.tensor_scalar(slot_used[:, :], p_sa[:, 0:BLOCKS], 1.0, None, ALU.min).then_inc(step, 1)
                nc.vector.tensor_scalar(slot_a[:, :], p_sa[:, 0:BLOCKS], 0.0, EMPTY, ALU.is_equal, ALU.mult)\
                    .then_inc(step, 1)
                nc.vector.tensor_scalar(slot_b[:, :], p_sb[:, 0:BLOCKS], float(P), -1.0, ALU.mult, ALU.add)\
                    .then_inc(step, 1)
                dve.wait_ge(step, n + 3)
                nc.vector.tensor_tensor(slot_b[:, :], slot_b[:, :], p_sa[:, 0:BLOCKS], ALU.add).then_inc(step, 1)
                dve.wait_ge(step, n + 4)
                nc.vector.tensor_tensor(slot_b[:, :], slot_b[:, :], slot_a[:, :], ALU.add).then_inc(step, 1)
                dve.wait_ge(step, n + 5)
                nc.vector.tensor_copy(slot_row[:, :], slot_b[:, :]).then_inc(done, 1)

            make_table(t_step, 0, tab_ready)

            dve.wait_ge(e_one, 3 * TILES)
            nc.vector.reduce_max(top[:, :], ranks[:, :], axis=mybir.AxisListType.X).then_inc(lv_top, 1)
            dve.wait_ge(lv_row, 1)
            nc.vector.reduce_max(levf[:, :], p_cum[0:1, 0:P], axis=mybir.AxisListType.X).then_inc(lv_top, 1)
            dve.wait_ge(lv_top, 2)
            nc.vector.tensor_scalar(levi[:, :], levf[:, :], float(P), None, ALU.add).then_inc(lv_top, 1)
            dve.wait_ge(lv_top, 3)
            nc.vector.tensor_scalar(levels[:, :], levi[:, :], 7, None, ALU.arith_shift_right).then_inc(lv_ready, 1)
            dve.wait_ge(lv_ready, 1)
            n_levels = dve.value_load(levels[0:1, 0:1], min_val=1, max_val=TILES)
            with dve.If(n_levels > 1):
                nc.vector.memset(put[:, :].bitcast(f32), 0.0).then_inc(v_zero, 1)
                dve.wait_ge(v_zero, 1)
                nc.vector.tensor_copy(put[:, LOC:LOC + 1], cst[:, C_PART:C_PART + 1]).then_inc(v_zero, 1)
                with dve.Fori(0, n_levels) as lv:
                    with dve.Fori(0, TILES) as t:
                        dve.wait_ge(v_tab, lv * TILES + t + 1)
                        nc.vector.tensor_scalar(ohb[:, 0, :], blocks[:, :], blkf[:, bass.ds(t, 1)], None,
                                                ALU.is_equal).then_inc(v_oh, 1)
                        nc.vector.tensor_scalar(oha[:, 0, :], iota[:, :], ranks[:, bass.ds(t, 1)],
                                                cst[:, C_PART:C_PART + 1], ALU.is_equal, ALU.mult).then_inc(v_oh, 1)
                        nc.vector.tensor_scalar(oht[:, 0, :], iota[:, :], ranks[:, bass.ds(t, 1)],
                                                cst[:, bass.ds(C_TILE + t, 1)], ALU.is_equal, ALU.mult)\
                            .then_inc(v_oh, 1)
                    dve.wait_ge(v_tab, lv * TILES + TILES + 1)
                    make_table(v_step, lv * 6, v_rows)
                    nc.vector.tensor_scalar(ranks[:, :], ranks[:, :], float(-P), None, ALU.add).then_inc(v_step, 1)
                    need_apart(dve, dve_passed, v_step, lv * 6 + 6)
                    with dve.Fori(0, BLOCKS) as b:
                        n = lv * BLOCKS + b
                        dve.wait_ge(v_got, n * 16 + 16)
                        nc.vector.tensor_scalar(oh[:, 0, :], iota1[:, :], mg[:, 0, LOC:LOC + 1].bitcast(f32),
                                                slot_used[:, bass.ds(b, 1)], ALU.is_equal, ALU.mult)\
                            .then_inc(v_one, 1)
                        dve.wait_ge(v_sum, n + 2)
                        dve.wait_ge(v_prev, n * 16 + 16)
                        nc.vector.tensor_tensor(total[:, 0, :], pn_s[0][:, 0:SUMMED],
                                                before[:, 0:SUMMED].bitcast(f32), ALU.add).then_inc(v_acc, 1)
                        dve.wait_ge(v_acc, n * 3 + 1)
                        nc.vector.tensor_tensor(total[:, 1, :], total[:, 0, :],
                                                before[:, HALF:HALF + SUMMED].bitcast(f32), ALU.add)\
                            .then_inc(v_acc, 1)
                        dve.wait_ge(v_acc, n * 3 + 2)
                        nc.vector.tensor_copy(put[:, 0:SUMMED], total[:, 1, :]).then_inc(v_acc, 1)
                        dve.wait_ge(v_acc, n * 3 + 3)
                        nc.vector.tensor_tensor(put[:, HALF:HALF + SUMMED], total[:, 1, :],
                                                put[:, 0:SUMMED].bitcast(f32), ALU.subtract).then_inc(v_add, 1)
                nc.vector.memset(slot_used[:, :], 1.0).then_inc(tab_ready, 1)
                dve.wait_ge(tab_ready, 2)

            def one_hot(j, u):
                need(dve, S["n_seg"], j - 3)
                dve.wait_ge(got_m[u % 4], 16 * (uses(j, NU, u) * 2 + u // 4 + 1))
                nc.vector.tensor_scalar(oh[:, u % 4, :], iota1[:, :], mg[:, u % 4, LOC:LOC + 1].bitcast(f32),
                                        slot_used[:, bass.ds(j, 1)], ALU.is_equal, ALU.mult).then_inc(S["n_oh"], 1)

            def gated_h(j, u):
                dve.wait_ge(S["n_rz"], j + 1)
                nc.vector.tensor_tensor(rhn[:, u % 2, :], rz[:, u % 4, 0:D], pn_n[u % 2][:, 0:D], ALU.mult)\
                    .then_inc(S["n_rhn"], 1)

            def n_input(j, u):
                dve.wait_ge(S["n_rhn"], j + 1)
                need(dve, S["n_tanh"], j - 1)
                nc.vector.tensor_tensor(npre[:, u % 2, :], rhn[:, u % 2, :], pn_n[u % 2][:, D:2 * D], ALU.add)\
                    .then_inc(S["n_npre"], 1)

            def x_lo(j, u):
                dve.wait_ge(S["n_xh"], j + 1)
                nc.vector.tensor_tensor(xl[:, u % 4, :], pn_t[u % 2][:, 0:D], xh[:, u % 4, :].bitcast(f32),
                                        ALU.subtract).then_inc(S["n_xl"], 1)

            def s_lo(j, u):
                dve.wait_ge(S["n_sh"], j + 1)
                nc.vector.tensor_tensor(sl[:, u % 2, :], pn_t[u % 2][:, D:2 * D], sh[:, u % 2, :].bitcast(f32),
                                        ALU.subtract).then_inc(S["n_sl"], 1)

            def count_eps(j, u):
                dve.wait_ge(S["n_seg"], j + 1)
                nc.vector.tensor_scalar(cnt_eps[:, u % 4:u % 4 + 1], pn_s[u % 2][:, CNT:CNT + 1], EPS_CNT, None,
                                        ALU.add).then_inc(S["n_ce"], 1)

            def count_inv(j, u):
                dve.wait_ge(S["n_ce"], j + 1)
                need(dve, S["n_mean"], j - 3)
                nc.vector.reciprocal(rcount[:, u % 4:u % 4 + 1], cnt_eps[:, u % 4:u % 4 + 1]).then_inc(S["n_rc"], 1)

            def z_diff(j, u):
                dve.wait_ge(S["n_diff"], j + 1)
                nc.vector.tensor_tensor(zd[:, u % 2, :], rz[:, u % 4, D:2 * D], diff[:, u % 4, :], ALU.mult)\
                    .then_inc(S["n_zd"], 1)

            def x_new(j, u):
                dve.wait_ge(S["n_zd"], j + 1)
                nc.vector.tensor_tensor(xn[:, u % 2, :], zd[:, u % 2, :], nt[:, u % 4, :], ALU.add)\
                    .then_inc(S["n_xn"], 1)

            def stats(j, u, tile, before, st, done):
                dve.wait_ge(before, j + 1)
                nc.vector.bn_stats(st[:, u % 4, :], tile).then_inc(done, 1)

            def aggregate(j, u, before, st, ag, done):
                need_apart(dve, dve_passed, before, j + 1)
                nc.vector.bn_aggr(ag[:, u % 4, :], st[:, u % 4, :]).then_inc(done, 1)

            def var_eps(j, u, before, ag, ve, done):
                dve.wait_ge(before, j + 1)
                nc.vector.tensor_scalar(ve[:, u % 4:u % 4 + 1], ag[:, u % 4, 1:2], EPS_LN, None, ALU.add)\
                    .then_inc(done, 1)

            def scale_gamma(j, u):
                dve.wait_ge(S["n_a1"], j + 1)
                nc.vector.scalar_tensor_tensor(out=tg[:, u % 2, :], in0=xn[:, u % 2, :], scalar=ag1[:, u % 4, 0:1],
                                               in1=gammab[:, :], op0=ALU.subtract, op1=ALU.mult)\
                    .then_inc(S["n_tg"], 1)

            def residual(j, u):
                dve.wait_ge(S["n_tg"], j + 1)
                dve.wait_ge(S["n_r1"], j + 1)
                dve.wait_ge(S["n_xb"], j + 1)
                need(dve, S["n_y"], j - 3)
                nc.vector.scalar_tensor_tensor(out=uu[:, u % 4, :], in0=tg[:, u % 2, :],
                                               scalar=rs1[:, u % 4:u % 4 + 1], in1=xb[:, u % 4, :],
                                               op0=ALU.mult, op1=ALU.add).then_inc(S["n_u"], 1)

            def minus_mean(j, u):
                dve.wait_ge(S["n_r2"], j + 1)
                nc.vector.tensor_scalar(nmr[:, u % 4:u % 4 + 1], ag2[:, u % 4, 0:1], rs2[:, u % 4:u % 4 + 1], -1.0,
                                        ALU.mult, ALU.mult).then_inc(S["n_nmr"], 1)

            parts = [
                (gated_h, -1), (x_lo, 2), (n_input, -1), (z_diff, -2), (residual, -3), (count_eps, 2),
                (minus_mean, -4),
                (x_new, -2), (count_inv, 2),
                (lambda j, u: stats(j, u, uu[:, u % 4, :], S["n_u"], st2, S["n_s2"]), -3),
                (s_lo, 1),
                (lambda j, u: stats(j, u, xn[:, u % 2, :], S["n_xn"], st1, S["n_s1"]), -2),
                (lambda j, u: aggregate(j, u, S["n_s2"], st2, ag2, S["n_a2"]), -3),
                (one_hot, 3),
                (lambda j, u: aggregate(j, u, S["n_s1"], st1, ag1, S["n_a1"]), -2),
                (lambda j, u: var_eps(j, u, S["n_a2"], ag2, ve2, S["n_v2"]), -3),
                (lambda j, u: var_eps(j, u, S["n_a1"], ag1, ve1, S["n_v1"]), -2),
                (scale_gamma, -2),
            ]

            def turn(i):
                for u in range(NU):
                    for part, lag in parts:
                        if not isinstance(i, int) or 0 <= i + u + lag < BLOCKS:
                            part(i + u + lag, (u + lag) % NU)

            turn(-NU)
            turn(0)
            with dve.Fori(1, BLOCKS // NU - 1) as g:
                turn(g * NU)
            turn(BLOCKS - NU)
            turn(BLOCKS)

        @block.tensor
        def _(pe):
            def mm(out_, lhsT, rhs, start, stop, skip=False):
                return nc.tensor.matmul(out_, lhsT, rhs, start=start, stop=stop, skip_group_check=skip)

            pe.wait_ge(ld_e, 48)
            pe.wait_ge(ld_w, 16 * (W_LOADS - 1))
            pe.wait_ge(w_step, 3)
            one2 = cst[0:1, C_SEL4 + 2:C_SEL4 + 4]
            mm(pe_m[0][0:2, 0:D], one2, brow[:, 6 * D:7 * D], True, True).then_inc(setup_mm, 1)
            for i in range(KC):
                need(pe, setup_cp, 2 * i)
                for bank, n0, n1 in ((p_sa, 0, 2 * D), (p_sb, 2 * D, 3 * D)):
                    for o in range(KC):
                        last = mm(bank[:, 0:n1 - n0], w2s[:, o, i * P:(i + 1) * P], wih[:, o, n0:n1],
                                  o == 0, o == KC - 1)
                last.then_inc(setup_mm, 1)
            pe.wait_ge(setup_cp, 2 * KC)
            sel = cst[0:1, C_SEL4:C_SEL4 + 4]
            for o in range(KC):
                mm(p_sa[0:4, :], b2s[:, o, :], wih[:, o, 0:2 * D], o == 0, False)
            mm(p_sa[0:4, :], sel, brow[:, 0:2 * D], False, False)
            mm(p_sa[0:4, :], sel, brow[:, 3 * D:5 * D], False, True)
            mm(p_sb[0:4, 0:D], sel, brow[:, 5 * D:6 * D], True, True)
            for o in range(KC):
                mm(p_sb[0:4, D:2 * D], b2s[:, o, :], wih[:, o, 2 * D:3 * D], o == 0, False)
            mm(p_sb[0:4, D:2 * D], sel, brow[:, 2 * D:3 * D], False, True).then_inc(setup_mm, 1)

            def edge_transpose(t, u):
                pe.wait_ge(got_src[u], 16 * (uses(t, EU, u) + 1))
                pe.wait_ge(got_dst[u], 16 * (uses(t, EU, u) + 1))
                need(pe, e_lo, t - 1)
                for c in range(2 * KC):
                    tile = (xsrc if c < KC else xdst)[:, u, (c % KC) * P:(c % KC + 1) * P]
                    last = nc.tensor.transpose(pe_t[u % 2][:, c * P:(c + 1) * P], tile, ident)
                last.then_inc(e_xt, 1)

            def edge_earlier(t, u, first=False):
                pe.wait_ge(e_oh, t + 1)
                mm(p_cum[:, 0:BLOCKS], lower[:, :], ohb[:, u % 2, :], first, True, True).then_inc(e_cum, 1)

            def edge_products(t, u):
                pe.wait_ge(e_lo, t + 1)
                need(pe, e_msg, t - 1)
                o = pe_m[u % 2][:, 0:D]
                for c in range(2 * KC):
                    h, l = (a[:, u % 2, c * P:(c + 1) * P] for a in (eh, el))
                    mm(o, h, w1h[:, c, :], c == 0, False)
                    mm(o, h, w1l[:, c, :], False, False)
                    mm(o, l, w1h[:, c, :], False, False)
                mm(o, ones[:, :], bias1[:, :], False, True).then_inc(e_mm, 1)

            def edge_table(t, u, first=False):
                pe.wait_ge(e_rank, t + 1)
                mm(p_cum[:, 0:BLOCKS], upto[:, :], ohb[:, u % 2, :], False, True, True)
                pe.wait_ge(e_one, 3 * t + 2)
                mm(p_sa[:, 0:BLOCKS], oha[:, u % 2, :], ohb[:, u % 2, :], first, True, True)
                mm(p_sb[:, 0:BLOCKS], oht[:, u % 2, :], ohb[:, u % 2, :], first, True, True).then_inc(e_tab, 1)

            pe.wait_ge(w_split, 3)
            pe.wait_ge(setup_cp, 2 * KC + 2)
            edge_transpose(0, 0)

            def edge_turn(t0, more=True, first=False):
                for u in range(EU):
                    t = t0 + u
                    edge_earlier(t, u, first and u == 0)
                    if more or u + 1 < EU:
                        edge_transpose(t0 + (u + 1), (u + 1) % EU)
                    edge_products(t, u)
                    edge_table(t, u, first and u == 0)

            edge_turn(0, first=True)
            with pe.Fori(1, TILES // EU - 1) as g:
                edge_turn(g * EU)
            edge_turn(TILES - EU, more=False)

            def segment_products(bank, one_hots, rows):
                mm(bank[:, 0:SUMMED], one_hots, rows[:, 0:SUMMED], True, False)
                return mm(bank[:, 0:SUMMED], one_hots, rows[:, HALF:HALF + SUMMED], False, True)

            pe.wait_ge(e_msg, TILES)
            pe.wait_ge(e_lo, TILES)
            pe.wait_ge(tab_ready, 1)

            pe.wait_ge(lv_top, 1)
            mm(p_cum[0:1, 0:P], top[:, :], ident, True, True).then_inc(lv_row, 1)
            pe.wait_ge(lv_ready, 1)
            n_levels = pe.value_load(levels[0:1, 0:1], min_val=1, max_val=TILES)
            with pe.If(n_levels > 1):
                pe.sem_inc(v_tab)
                pe.sem_inc(v_sum)
                with pe.Fori(0, n_levels) as lv:
                    def level_tile(t, first):
                        pe.wait_ge(v_oh, (lv * TILES + t) * 3 + 3)
                        mm(p_sa[:, 0:BLOCKS], oha[:, 0, :], ohb[:, 0, :], first, True, True)
                        mm(p_sb[:, 0:BLOCKS], oht[:, 0, :], ohb[:, 0, :], first, True, True).then_inc(v_tab, 1)
                    level_tile(0, True)
                    with pe.Fori(1, TILES) as t:
                        level_tile(t, False)
                    with pe.Fori(0, BLOCKS) as b:
                        pe.wait_ge(v_one, lv * BLOCKS + b + 1)
                        segment_products(pn_s[0], oh[:, 0, :], mg[:, 0, :]).then_inc(v_sum, 1)

            def x_transpose(j, u):
                pe.wait_ge(got_x[u], 16 * (uses(j, NU, u) + 1))
                need(pe, S["n_sl"], j - 1)
                for c in range(KC):
                    last = nc.tensor.transpose(pn_t[u % 2][:, c * P:(c + 1) * P], xs[:, u, c * P:(c + 1) * P], ident)
                last.then_inc(S["n_xt"], 1)

            def s_transpose(j, u):
                pe.wait_ge(S["n_mean"], j + 1)
                pe.wait_ge(S["n_xl"], j + 1)
                for c in range(KC):
                    nc.tensor.transpose(pn_t[u % 2][:, D + c * P:D + (c + 1) * P],
                                        mean[:, u % 2, c * P:(c + 1) * P], ident)
                nc.tensor.transpose(pn_s[u % 2][0:4, 384:384 + P], mean[:, u % 2, D:D + 4], ident)\
                    .then_inc(S["n_st"], 1)

            def segment_sum(j, u):
                pe.wait_ge(S["n_oh"], j + 1)
                need(pe, S["n_has"], j - 1)
                segment_products(pn_s[u % 2], oh[:, u % 4, :], mg[:, u % 4, :]).then_inc(S["n_seg"], 1)

            def products(j, u):
                pe.wait_ge(S["n_xl"], j + 1)
                pe.wait_ge(S["n_sl"], j + 1)
                pe.wait_ge(S["n_has"], j + 1)
                need(pe, S["n_npre"], j - 1)
                o_rz, o_h, o_i = pn_rz[u % 2][:, :], pn_n[u % 2][:, 0:D], pn_n[u % 2][:, D:2 * D]

                def part(o, h, l, wh, wl, n0, n1, first):
                    for c in range(KC):
                        a, b = h[:, c * P:(c + 1) * P], l[:, c * P:(c + 1) * P]
                        mm(o, a, wh[:, c, n0:n1], first and c == 0, False)
                        mm(o, a, wl[:, c, n0:n1], False, False)
                        mm(o, b, wh[:, c, n0:n1], False, False)
                x_, s_ = (xh[:, u % 4, :], xl[:, u % 4, :], wxh, wxl), (sh[:, u % 2, :], sl[:, u % 2, :], wsh, wsl)
                has = hasrow[:, u % 2, :]
                part(o_rz, *x_, 0, 2 * D, True)
                part(o_rz, *s_, 0, 2 * D, False)
                mm(o_rz, has, bias[:, 0:2 * D], False, True)
                part(o_h, *x_, 2 * D, 3 * D, True)
                mm(o_h, has, bias[:, 2 * D:3 * D], False, True)
                part(o_i, *s_, 2 * D, 3 * D, True)
                mm(o_i, has, bias[:, 3 * D:4 * D], False, True).then_inc(S["n_mm"], 1)

            def turn(i):
                for u in range(NU):
                    for part, lag in ((x_transpose, 2), (s_transpose, 1), (segment_sum, 2), (products, 0)):
                        if not isinstance(i, int) or 0 <= i + u + lag < BLOCKS:
                            part(i + u + lag, (u + lag) % NU)

            turn(-NU)
            turn(0)
            with pe.Fori(1, BLOCKS // NU - 1) as g:
                turn(g * NU)
            turn(BLOCKS - NU)


def kernel(x, src, dst, L0_gnn_W1, L0_gnn_b1, L0_gnn_W2, L0_gnn_b2, L0_gnn_w_ih, L0_gnn_w_hh,
           L0_gnn_b_ih, L0_gnn_b_hh, L0_gnn_gamma, L0_gnn_beta):
    import concourse.bacc as bacc
    from concourse.bass_utils import run_bass_kernel_spmd

    def arr(a):
        return np.ascontiguousarray(np.asarray(a))
    x, src, dst = arr(x), arr(src), arr(dst)
    xp = np.zeros((NODES_PAD, D), x.dtype)
    xp[:NODES] = x
    pad = EDGES_PAD - EDGES
    srcp = np.concatenate([src, ((BLOCKS - 1) * P + np.arange(pad)).astype(src.dtype)])
    dstp = np.concatenate([dst, np.zeros(pad, dst.dtype)])
    ins = {
        "x": xp, "src": srcp, "dst": dstp, "w1t": arr(arr(L0_gnn_W1).T), "b1": arr(L0_gnn_b1),
        "w2": arr(L0_gnn_W2), "b2": arr(L0_gnn_b2), "wiht": arr(arr(L0_gnn_w_ih).T),
        "whht": arr(arr(L0_gnn_w_hh).T), "bih": arr(L0_gnn_b_ih), "bhh": arr(L0_gnn_b_hh),
        "gamma": arr(L0_gnn_gamma), "beta": arr(L0_gnn_beta), "consts": constants(),
    }
    nc = bacc.Bacc("TRN2", target_bir_lowering=False, num_devices=1)
    arrays, args = {}, []
    for name, a in ins.items():
        arrays[f"in_{name}"] = a
        args.append(nc.dram_tensor(f"in_{name}", a.shape, mybir.dt.from_np(a.dtype), kind="ExternalInput").ap())
    args.append(nc.dram_tensor("out_y", (NODES_PAD, D), mybir.dt.float32, kind="ExternalOutput").ap())
    gnn_layer(nc, *args)
    r = run_bass_kernel_spmd(nc, [arrays], core_ids=[0])
    return r.results[0]["out_y"][:NODES]
```

```python
from contextlib import ExitStack

import numpy as np

import concourse.bass as bass
from concourse import mybir

P = 128
D = 256
KC = D // P
NODES = 50000
EDGES = 25000
BLOCKS = 392
PAIRS = BLOCKS // 2
NODES_PAD = BLOCKS * P
TILES = 196
EDGES_PAD = TILES * P
EU = 4
QU = 4
TURNS = PAIRS // QU
BROWS = 34
CNT = D
LOC = D + 2
SUMMED = D + 2
HALF = D + 4
ROW = 2 * HALF
EMPTY = float(1 << 20)
T_LOW = 8
CODE_EXP = 127 + 10 - 24
EPS_LN = 1e-5
EPS_CNT = 1e-8

C_IDENT, C_LOWER, C_UPTO, C_IOTA = 0, P, 2 * P, 3 * P
C_BLOCK = 4 * P
C_CODE = C_BLOCK + BLOCKS
C_PART = C_CODE + TILES
C_LO1 = C_PART + 1
C_LO4 = C_LO1 + 1
C_SEL = C_LO4 + 1
C_ALL = C_SEL + BROWS


def constants():
    c = np.zeros((P, C_ALL), np.float32)
    i = np.arange(P)
    c[:, C_IDENT:C_IDENT + P] = np.eye(P)
    c[:, C_LOWER:C_LOWER + P] = i[:, None] < i[None, :]
    c[:, C_UPTO:C_UPTO + P] = i[:, None] >= i[None, :]
    c[:, C_IOTA:C_IOTA + P] = i[None, :]
    c[:, C_BLOCK:C_BLOCK + BLOCKS] = np.arange(BLOCKS)[None, :]
    t = np.arange(TILES)[None, :]
    c[:, C_CODE:C_CODE + TILES] = (1024 + i[:, None] * T_LOW + t % T_LOW) * 2.0 ** (t // T_LOW - 24)
    c[:, C_PART] = i + 1
    c[:, C_LO1] = np.where(i == 1, -1, 0)
    c[:, C_LO4] = np.where((i == 1) | (i == 33), -1, 0)
    c[:, C_SEL + 32:C_SEL + BROWS] = 1
    return c


def gnn_layer(nc, x, xt, src, dst, w1t, b1, w2, b2, wiht, whht, bih, bhh, gamma, beta, consts, out):
    f32, f32r, bf16, i32 = mybir.dt.float32, mybir.dt.float32r, mybir.dt.bfloat16, mybir.dt.int32
    fp16 = mybir.dt.float16
    ACT, ALU = mybir.ActivationFunctionType, mybir.AluOpType
    ctx = ExitStack()
    with ctx:
        def sb(name, shape, dt=f32, until=ctx):
            return until.enter_context(nc.sbuf_tensor(name, shape, dt))

        def sem(name):
            return ctx.enter_context(nc.semaphore(name))

        def sems(name, n):
            return [sem(f"{name}{i}") for i in range(n)]

        messages = nc.dram_tensor("messages", [EDGES_PAD, ROW], f32, kind="Internal").ap()
        sums = nc.dram_tensor("sums", [NODES_PAD, ROW], f32, kind="Internal").ap()

        cst = sb("cst", [P, C_ALL])
        ident = cst[:, C_IDENT:C_IDENT + P]
        lower = sb("lower", [P, P], fp16)
        upto = sb("upto", [P, P], fp16)
        iota = sb("iota", [P, P], fp16)
        blocks = sb("blocks", [P, BLOCKS], fp16)
        iota1 = sb("iota1", [P, P])
        srci = sb("srci", [P, TILES], i32)
        dsti = sb("dsti", [P, TILES], i32)
        blkf = sb("blkf", [P, TILES])
        locf = sb("locf", [P, TILES])
        ranks = sb("ranks", [P, TILES])
        slot_row = sb("slot_row", [P, BLOCKS], i32)
        slot_used = sb("slot_used", [P, BLOCKS])
        wxh, wxl = sb("wxh", [P, KC, 3 * D], f32r), sb("wxl", [P, KC, 3 * D], f32r)
        wsh, wsl = sb("wsh", [P, KC, 3 * D], f32r), sb("wsl", [P, KC, 3 * D], f32r)
        bias = sb("bias", [P, 4 * D], f32r)
        ones = sb("ones", [P, P], f32r)
        gammab, betab = sb("gammab", [P, D]), sb("betab", [P, 2 * D])

        XE = 4
        src_now, dst_now = sb("src_now", [P, 2, EU], i32), sb("dst_now", [P, 2, EU], i32)
        rows_now = sb("rows_now", [P, 2 * QU], i32)
        msg = sb("msg", [P, EU, ROW], f32r)
        ohb = sb("ohb", [P, 2, BLOCKS], fp16)
        rank = sb("rank", [P, 2])
        oha = sb("oha", [P, 2, P], fp16)

        mg = sb("mg", [P, QU, 2, ROW], f32r)
        oh = sb("oh", [P, QU, 2, P], f32r)
        hasrow = sb("hasrow", [P, QU, 2, P], f32r)
        halves = sb("halves", [P, 2])

        top, levf, levi = sb("top", [P, 1]), sb("levf", [1, 1]), sb("levi", [1, 1], i32)
        levels = sb("levels", [1, 1], i32)

        early = ExitStack()
        before, total = sb("before", [P, ROW], f32r, until=early), sb("total", [P, 2, SUMMED], until=early)
        put = sb("put", [P, ROW], f32r, until=early)
        slot_bits, slot_parts = sb("slot_bits", [P, 3, BLOCKS], i32, until=early), sb("slot_parts", [P, 4, BLOCKS], until=early)
        parity, place, pairi, loci = (sb(n, [P, TILES], i32, until=early) for n in ("parity", "place", "pairi", "loci"))
        pairf, parityf = sb("pairf", [P, TILES], until=early), sb("parityf", [P, TILES], until=early)
        w1h, w1l = (sb(n, [P, 2 * KC, D], f32r, until=early) for n in ("w1h", "w1l"))
        stage = sb("stage", [P, 2 * KC, D], until=early)
        bias1, bias1h = (sb(n, [P, D], f32r, until=early) for n in ("bias1", "bias1h"))
        xsrc, xdst = (sb(n, [P, XE, D], until=early) for n in ("xsrc", "xdst"))
        eh, el = (sb(n, [P, 2, 2 * KC * P], f32r, until=early) for n in ("eh", "el"))
        sil = sb("sil", [P, 2, D], until=early)
        w2s, b2s = sb("w2s", [P, KC, D], until=early), sb("b2s", [P, KC, BROWS], until=early)
        brow = sb("brow", [1, 3 * D + 3 * D + D], until=early)
        picked = sb("picked", [P, BLOCKS], fp16, until=early)
        wih, whh = (sb(n, [P, KC, 3 * D], until=early) for n in ("wih", "whh"))
        biash = sb("biash", [BROWS, 4 * D], f32r, until=early)
        early.close()

        xs, xts = sb("xs", [P, QU, 2 * D]), sb("xts", [P, QU, 2 * D])
        xh, xl = sb("xh", [P, QU, 2 * D], f32r), sb("xl", [P, QU, 2 * D], f32r)
        mean = sb("mean", [P, 2, 2, D])
        sh, sl = sb("sh", [P, 2, 2 * D], f32r), sb("sl", [P, 2, 2 * D], f32r)
        xb = sb("xb", [P, QU, 2 * D])
        cnt_eps, rcount = sb("cnt_eps", [P, QU, 2]), sb("rcount", [P, QU, 2])
        rz = sb("rz", [P, QU, 2, 2 * D])
        rhn, npre = sb("rhn", [P, 2, 2, D]), sb("npre", [P, 2, 2 * D])
        nt, diff = sb("nt", [P, QU, 2 * D]), sb("diff", [P, QU, 2 * D])
        zd, xn = sb("zd", [P, 2, 2 * D]), sb("xn", [P, 2, 2 * D])
        st1, ag1 = sb("st1", [P, QU, 2, 6]), sb("ag1", [P, QU, 2, 2])
        st2, ag2 = sb("st2", [P, QU, 2, 6]), sb("ag2", [P, QU, 2, 2])
        ve1, ve2, rs1, rs2, nmr = (sb(n, [P, QU, 2]) for n in ("ve1", "ve2", "rs1", "rs2", "nmr"))
        tg, uu, yy = sb("tg", [P, 2, 2 * D]), sb("uu", [P, QU, 2 * D]), sb("yy", [P, QU, 2 * D])

        pairs_of_banks = [ctx.enter_context(nc.psum_tensor(f"banks{i}", [P, 2, 512], f32)) for i in range(4)]
        pe_t, pe_m = pairs_of_banks[0], pairs_of_banks[1]
        p_cum, p_tab = pairs_of_banks[2][:, 0, :], pairs_of_banks[2][:, 1, :]
        p_wc, p_bias = pairs_of_banks[0:2], pairs_of_banks[3]
        pn_t, pn_s, pn_rz, pn_n = pairs_of_banks

        ld_w1, ld_w = sem("ld_w1"), sem("ld_w")
        ld_e, ld_c = sem("ld_e"), sem("ld_c")
        cst_ready, w_split, setup_mm, setup_cp, idx_ready = (
            sem("cst_ready"), sem("w_split"), sem("setup_mm"), sem("setup_cp"), sem("idx_ready"))
        w1_hi, b1_mm, b1_hi, w_hi = sem("w1_hi"), sem("b1_mm"), sem("b1_hi"), sem("w_hi")
        has_zero, node_ready = sem("has_zero"), sem("node_ready")
        got_src, got_dst, e_stored = sems("got_src", XE), sems("got_dst", XE), sems("e_stored", EU)
        e_xt, e_hi, e_lo, e_mm, e_msg, e_loc = (sem(n) for n in ("e_xt", "e_hi", "e_lo", "e_mm", "e_msg", "e_loc"))
        e_mh, e_ml = sem("e_mh"), sem("e_ml")
        e_oh, e_cum, e_rank, e_one, e_tab = (sem(n) for n in ("e_oh", "e_cum", "e_rank", "e_one", "e_tab"))
        idx_now = sem("idx_now")
        pool_passed, dve_passed, sp_passed = sem("pool_passed"), sem("dve_passed"), sem("sp_passed")
        t_step, tab_ready = sem("t_step"), sem("tab_ready")
        lv_top, lv_row, lv_ready = sem("lv_top"), sem("lv_row"), sem("lv_ready")
        v_zero, v_oh, v_tab, v_step, v_rows = (sem(n) for n in ("v_zero", "v_oh", "v_tab", "v_step", "v_rows"))
        v_idx, v_got, v_one, v_sum, v_prev = (sem(n) for n in ("v_idx", "v_got", "v_one", "v_sum", "v_prev"))
        v_acc, v_add, v_put, v_done = (sem(n) for n in ("v_acc", "v_add", "v_put", "v_done"))
        got_x, got_xt, got_m, n_stored = sems("got_x", QU), sems("got_xt", QU), sems("got_m", 2 * QU), sems("n_stored", QU)
        names = ("n_oh n_xh n_xl n_seg n_ce n_rc n_mean n_st n_sh n_has n_sl n_mm0 n_mm n_rz0 n_rz n_rhn n_npre n_tanh"
                 " n_diff n_xb n_zd n_xn n_s1 n_a1 n_v1 n_r1 n_tg n_u n_s2 n_a2 n_v2 n_r2 n_nmr n_y").split()
        S = {n: sem(n) for n in names}

        def need(eng, s, value):
            if not isinstance(value, int) or value > 0:
                eng.wait_ge(s, value)

        def need_apart(eng, passed, s, value):
            need(eng, s, value)
            eng.sem_inc(passed)

        def uses(j, slots, u):
            return j // slots if isinstance(j, int) else (j - u) // slots

        def node_turns(eng, parts, first, last):
            def step(q, u):
                for part, lag in parts:
                    if not isinstance(q, int) or 0 <= q + lag < PAIRS:
                        part(q + lag, (u + lag) % QU)

            head = QU * (-(min(lag for _, lag in parts) // QU) + 1)
            tail = PAIRS - QU * -(-max(lag for _, lag in parts) // QU)
            for q in range(first, head):
                step(q, q % QU)
            with eng.Fori(head // QU, tail // QU) as g:
                for u in range(QU):
                    step(g * QU + u, u)
            for q in range(tail, PAIRS + last):
                step(q, q % QU)

        def edges_done(eng):
            eng.wait_ge(e_mm, TILES)
            eng.wait_ge(e_ml, TILES)

        block = ctx.enter_context(nc.Block())
        W_LOADS = 12
        WC_PARTS = 2 * KC + 2

        @block.sync
        def _(sp):
            loads = [(srci[:, :], src.rearrange("(p t) -> p t", p=P)),
                     (dsti[:, :], dst.rearrange("(p t) -> p t", p=P)), (cst[:, :], consts)]
            for (a, b), done in zip(loads, (ld_e, ld_e, ld_c)):
                sp.dma_start(a, b).then_inc(done, 16)
            sp.dma_start(stage[:, :, :], w1t.rearrange("(k p) n -> p k n", p=P)).then_inc(ld_w1, 16)
            sp.dma_start(brow[:, 6 * D:7 * D], b1.rearrange("(a n) -> a n", a=1)).then_inc(ld_w1, 16)
            more = [(wih[:, :, :], wiht.rearrange("(k p) n -> p k n", p=P)),
                    (w2s[:, :, :], w2.rearrange("(k p) n -> p k n", p=P)),
                    (whh[:, :, :], whht.rearrange("(k p) n -> p k n", p=P)),
                    (brow[:, 0:3 * D], bih.rearrange("(a n) -> a n", a=1)),
                    (brow[:, 3 * D:6 * D], bhh.rearrange("(a n) -> a n", a=1)),
                    (gammab[:, :], gamma.rearrange("(a n) -> a n", a=1).to_broadcast([P, D])),
                    (betab[:, 0:D], beta.rearrange("(a n) -> a n", a=1).to_broadcast([P, D])),
                    (betab[:, D:2 * D], beta.rearrange("(a n) -> a n", a=1).to_broadcast([P, D]))]
            for k in range(KC):
                for c in range(2):
                    more.append((b2s[:, k, c:c + 1], b2[k * P:(k + 1) * P].rearrange("(p a) -> p a", a=1)))
            for a, b in more:
                sp.dma_start(a, b).then_inc(ld_w, 16)
            assert len(more) == W_LOADS

            def store_messages(t, u):
                sp.wait_ge(e_ml, t + 1)
                sp.wait_ge(e_loc, t + 1)
                sp.dma_start(messages[bass.ds(t * P, P), :], msg[:, u, :].bitcast(f32)).then_inc(e_stored[u], 16)

            for u in range(EU):
                store_messages(u, u)
            with sp.Fori(1, TILES // EU) as g:
                for u in range(EU):
                    store_messages(g * EU + u, u)

            sp.wait_ge(lv_ready, 1)
            n_levels = sp.value_load(levels[0:1, 0:1], min_val=1, max_val=TILES)
            with sp.If(n_levels > 1):
                sp.wait_ge(v_zero, 2)
                with sp.Fori(0, BLOCKS) as b:
                    sp.dma_start(sums[bass.ds(b * P, P), :], put[:, :].bitcast(f32)).then_inc(v_put, 16)
                    need_apart(sp, sp_passed, v_put, b * 16 + 16)
                with sp.Fori(0, n_levels) as lv:
                    with sp.Fori(0, BLOCKS) as b:
                        n = lv * BLOCKS + b
                        sp.dma_start(before[:, :].bitcast(f32), sums[bass.ds(b * P, P), :]).then_inc(v_prev, 16)
                        need_apart(sp, sp_passed, v_add, n + 1)
                        sp.dma_start(sums[bass.ds(b * P, P), :], put[:, :].bitcast(f32)).then_inc(v_put, 16)
                        need_apart(sp, sp_passed, v_put, n * 16 + 16 * (BLOCKS + 1))
                sp.sem_inc(v_done)

            x_pairs = x.rearrange("(r h) d -> r (h d)", h=2)
            out_pairs = out.rearrange("(r h) d -> r (h d)", h=2)

            def load_x(q, u):
                need(sp, S["n_xl"], q - QU + 1)
                sp.dma_start(xts[:, u, :], xt[bass.ds(q * P, P), :]).then_inc(got_xt[u], 16)
                need(sp, S["n_diff"], q - QU + 1)
                need(sp, S["n_xb"], q - QU + 1)
                sp.dma_start(xs[:, u, :], x_pairs[bass.ds(q * P, P), :]).then_inc(got_x[u], 16)

            def store_y(q, u):
                sp.wait_ge(S["n_y"], q + 1)
                sp.dma_start(out_pairs[bass.ds(q * P, P), :], yy[:, u, :]).then_inc(n_stored[u], 16)

            edges_done(sp)
            sp.wait_ge(tab_ready, 1)
            node_turns(sp, ((load_x, 3), (store_y, -5)), first=-3, last=5)
            for s in range(QU):
                sp.wait_ge(n_stored[s], 16 * TURNS)

        def gather(dst_tile, table, rows, done, bound=None):
            nc.gpsimd.indirect_dma_start(
                out=dst_tile, out_offset=None, in_=rows,
                in_offset=bass.IndirectOffsetOnAxis(ap=table, axis=0),
                bounds_check=bound, oob_is_err=False).then_inc(done, 16)

        @block.gpsimd
        def _(pool):
            last_row = pool.to_reg(EDGES_PAD - 1)
            nc.gpsimd.memset(msg[:, :, 0:HALF].bitcast(f32), 1.0).then_inc(cst_ready, 1)
            nc.gpsimd.memset(msg[:, :, HALF:ROW].bitcast(f32), 0.0).then_inc(cst_ready, 1)
            pool.wait_ge(ld_e, 32)

            def gather_edges(t0, turn_no, side):
                if not isinstance(turn_no, int) or turn_no >= 2:
                    for u in range(EU):
                        pool.wait_ge(got_dst[u], 16 * (turn_no - 1))
                nc.gpsimd.tensor_copy(src_now[:, side, :], srci[:, bass.ds(t0, EU)]).then_inc(idx_now, 1)
                nc.gpsimd.tensor_copy(dst_now[:, side, :], dsti[:, bass.ds(t0, EU)]).then_inc(idx_now, 1)
                pool.wait_ge(idx_now, 2 * turn_no + 2)
                for u in range(EU):
                    need_apart(pool, pool_passed, e_xt, t0 + (u - XE + 1))
                    gather(xsrc[:, u, :], src_now[:, side, u:u + 1], x, got_src[u])
                    gather(xdst[:, u, :], dst_now[:, side, u:u + 1], x, got_dst[u])

            E_TURNS = TILES // EU
            gather_edges(0, 0, 0)
            nc.gpsimd.memset(mg[:, :, :, :].bitcast(f32), 0.0).then_inc(node_ready, 1)
            nc.gpsimd.memset(halves[:, :], -0.5).then_inc(node_ready, 1)
            nc.gpsimd.memset(hasrow[:, :, :, :].bitcast(f32), 0.0).then_inc(has_zero, 1)
            nc.gpsimd.memset(bias[:, :].bitcast(f32), 0.0).then_inc(node_ready, 1)
            nc.gpsimd.memset(b2s[:, :, 2:BROWS], 0.0).then_inc(node_ready, 1)
            pool.wait_ge(has_zero, 1)
            pool.wait_ge(node_ready, 4)
            nc.gpsimd.memset(hasrow[32:BROWS, :, :, :].bitcast(f32), 1.0).then_inc(node_ready, 1)
            pool.wait_ge(node_ready, 5)
            with pool.Fori(0, E_TURNS // 2) as g:
                for side in range(2):
                    gather_edges((g * 2 + (side + 1)) * EU, g * 2 + (side + 1), (side + 1) % 2)

            edges_done(pool)
            for u in range(EU):
                pool.wait_ge(e_stored[u], 16 * (TILES // EU))
            pool.wait_ge(tab_ready, 1)
            def node_stage(summed):
                def copy_rows(q, u):
                    need(pool, S["n_oh"], q - QU + 2)
                    nc.gpsimd.tensor_copy(rows_now[:, 2 * u:2 * u + 4], slot_row[:, bass.ds(2 * q, 4)])\
                        .then_inc(idx_now, 1)
                    pool.wait_ge(idx_now, 2 * E_TURNS + 1 + (q // 2 if isinstance(q, int) else (q - u) // 2 + u // 2))

                def gather_rows(q, u):
                    if u % 2 == 0 and not summed:
                        copy_rows(q, u)
                    for h in range(2):
                        to = mg[:, u, h, :].bitcast(f32)
                        need_apart(pool, pool_passed, S["n_seg"], q - QU + 1)
                        if summed:
                            nc.gpsimd.dma_start(to, sums[bass.ds((q * 2 + h) * P, P), :])\
                                .then_inc(got_m[2 * u + h], 16)
                        else:
                            gather(to, rows_now[:, 2 * u + h:2 * u + h + 1], messages, got_m[2 * u + h], last_row)

                def x_lo(q, u):
                    pool.wait_ge(S["n_xh"], q + 1)
                    need(pool, S["n_mm"], q - QU + 1)
                    nc.gpsimd.tensor_tensor(out=xl[:, u, :], in0=xts[:, u, :], in1=xh[:, u, :].bitcast(f32),
                                            op=ALU.subtract).then_inc(S["n_xl"], 1)

                def add_beta(q, u):
                    need(pool, S["n_u"], q - QU + 1)
                    pool.wait_ge(got_x[u], 16 * (uses(q, QU, u) + 1))
                    nc.gpsimd.tensor_tensor(out=xb[:, u, :], in0=xs[:, u, :], in1=betab[:, :], op=ALU.add)\
                        .then_inc(S["n_xb"], 1)

                def subtract_n(q, u):
                    need(pool, S["n_zd"], q - QU + 1)
                    pool.wait_ge(S["n_tanh"], q + 1)
                    nc.gpsimd.tensor_tensor(out=diff[:, u, :], in0=xs[:, u, :], in1=nt[:, u, :], op=ALU.subtract)\
                        .then_inc(S["n_diff"], 1)

                def inv_std(q, u, var, ve, free, rs, done):
                    pool.wait_ge(var, q + 1)
                    need(pool, free, q - QU + 1)
                    nc.gpsimd.tensor_tensor(out=rs[:, u, :], in0=ve[:, u, :], in1=halves[:, :], op=ALU.pow)\
                        .then_inc(done, 1)

                def inv_std1(q, u):
                    inv_std(q, u, S["n_v1"], ve1, S["n_u"], rs1, S["n_r1"])

                def inv_std2(q, u):
                    inv_std(q, u, S["n_v2"], ve2, S["n_y"], rs2, S["n_r2"])

                node_turns(pool, ((gather_rows, 4), (inv_std1, -3), (inv_std2, -4), (x_lo, 2), (add_beta, -1),
                                  (subtract_n, -1)), first=-4, last=4)

            pool.wait_ge(ld_w, 16 * (W_LOADS))
            pool.wait_ge(lv_ready, 1)
            n_levels = pool.value_load(levels[0:1, 0:1], min_val=1, max_val=TILES)
            with pool.If(n_levels > 1):
                with pool.Fori(0, n_levels) as lv:
                    with pool.Fori(0, BLOCKS) as b:
                        n = lv * BLOCKS + b
                        pool.wait_ge(v_rows, lv + 1)
                        pool.wait_ge(v_sum, n + 1)
                        nc.gpsimd.tensor_copy(rows_now[:, 0:1], slot_row[:, bass.ds(b, 1)]).then_inc(v_idx, 1)
                        need_apart(pool, pool_passed, v_idx, n + 1)
                        gather(mg[:, 0, 0, :].bitcast(f32), rows_now[:, 0:1], messages, v_got, last_row)
                pool.wait_ge(v_done, 1)
                pool.wait_ge(tab_ready, 2)
                node_stage(True)
            with pool.Else():
                node_stage(False)

        @block.scalar
        def _(act):
            def edge_hi(t, u):
                act.wait_ge(e_xt, t + 1)
                need(act, e_mm, t - 1)
                nc.scalar.activation(eh[:, u % 2, :], pe_t[:, u % 2, :], ACT.Copy).then_inc(e_hi, 1)

            def edge_silu(t, u):
                act.wait_ge(e_mm, t + 1)
                need(act, e_ml, t - 1)
                nc.scalar.activation(sil[:, u % 2, :], pe_m[:, u % 2, 0:D], ACT.Silu).then_inc(e_msg, 1)

            def edge_message_hi(t, u):
                act.wait_ge(e_msg, t + 1)
                need(act, e_stored[u], 16 * uses(t, EU, u))
                nc.scalar.activation(msg[:, u, 0:D], sil[:, u % 2, :], ACT.Copy).then_inc(e_mh, 1)

            act.wait_ge(ld_w1, 32)
            nc.scalar.activation(w1h[:, :, :], stage[:, :, :], ACT.Copy).then_inc(w1_hi, 1)
            edge_hi(0, 0)
            act.wait_ge(cst_ready, 2)
            for t in range(EU):
                edge_hi(t + 1, (t + 1) % EU)
                edge_silu(t, t)
                edge_message_hi(t, t)
            with act.Fori(1, TILES // EU - 1) as g:
                for u in range(EU):
                    edge_hi(g * EU + (u + 1), (u + 1) % EU)
                    edge_silu(g * EU + u, u)
                    edge_message_hi(g * EU + u, u)
            for t in range(TILES - EU, TILES):
                if t + 1 < TILES:
                    edge_hi(t + 1, (t + 1) % EU)
                edge_silu(t, t % EU)
                edge_message_hi(t, t % EU)

            def gates(q, u):
                act.wait_ge(S["n_mm0"], q + 1)
                need(act, S["n_zd"], q - QU + 1)
                nc.scalar.activation(rz[:, u, 0, :], pn_rz[:, 0, :], ACT.Sigmoid).then_inc(S["n_rz0"], 1)
                act.wait_ge(S["n_mm"], q + 1)
                nc.scalar.activation(rz[:, u, 1, :], pn_rz[:, 1, :], ACT.Sigmoid).then_inc(S["n_rz"], 1)

            def x_hi(q, u):
                act.wait_ge(got_xt[u], 16 * (uses(q, QU, u) + 1))
                need(act, S["n_mm"], q - QU + 1)
                nc.scalar.activation(xh[:, u, :], xts[:, u, :], ACT.Copy).then_inc(S["n_xh"], 1)

            def has_edges(q, u):
                act.wait_ge(S["n_seg"], q + 1)
                need(act, S["n_mm"], q - QU + 1)
                nc.scalar.activation(hasrow[0:2, u, :, :], pn_s[0:2, :, 384:384 + P], ACT.Sign)\
                    .then_inc(S["n_has"], 1)

            def mean_rows(q, u):
                act.wait_ge(S["n_rc"], q + 1)
                need(act, S["n_st"], q - 1)
                for h in range(2):
                    last = nc.scalar.activation(mean[:, u % 2, h, :], pn_s[:, h, 0:D], ACT.Copy,
                                                scale=rcount[:, u, h:h + 1])
                last.then_inc(S["n_mean"], 1)

            def s_hi(q, u):
                act.wait_ge(S["n_st"], q + 1)
                need(act, S["n_mm"], q - 1)
                nc.scalar.activation(sh[:, u % 2, :], pn_t[:, u % 2, :], ACT.Copy).then_inc(S["n_sh"], 1)

            def tanh(q, u):
                act.wait_ge(S["n_npre"], q + 1)
                need(act, S["n_xn"], q - QU + 1)
                nc.scalar.activation(nt[:, u, :], npre[:, u % 2, :], ACT.Tanh).then_inc(S["n_tanh"], 1)

            def last_norm(q, u):
                act.wait_ge(S["n_nmr"], q + 1)
                need(act, n_stored[u], 16 * uses(q, QU, u))
                for h in range(2):
                    last = nc.scalar.activation(yy[:, u, h * D:(h + 1) * D], uu[:, u, h * D:(h + 1) * D],
                                                ACT.Identity, bias=nmr[:, u, h:h + 1], scale=rs2[:, u, h:h + 1])
                last.then_inc(S["n_y"], 1)

            act.wait_ge(ld_w, 16 * W_LOADS)
            act.wait_ge(node_ready, 5)
            nc.scalar.activation(wxh[:, :, :], whh[:, :, :], ACT.Copy).then_inc(w_hi, 1)
            for k in range(KC):
                act.wait_ge(setup_mm, k + 1)
                for c, (n0, n1) in enumerate(((0, 2 * D), (2 * D, 3 * D))):
                    nc.scalar.activation(wsh[:, k, n0:n1], p_wc[k][:, c, 0:n1 - n0], ACT.Copy).then_inc(w_hi, 1)
            act.wait_ge(setup_mm, KC + 1)
            for c in range(2):
                nc.scalar.activation(biash[:, c * 2 * D:(c + 1) * 2 * D], p_bias[0:BROWS, c, :], ACT.Copy)\
                    .then_inc(w_hi, 1)
            edges_done(act)
            node_turns(act, ((gates, -1), (s_hi, 1), (x_hi, 2), (tanh, -1), (has_edges, 2), (mean_rows, 2),
                             (last_norm, -4)), first=-2, last=5)

        @block.vector
        def _(dve):
            dve.wait_ge(ld_e, 32)
            dve.wait_ge(ld_c, 16)
            steps = [
                lambda: nc.vector.tensor_copy(lower[:, :], cst[:, C_LOWER:C_LOWER + P]),
                lambda: nc.vector.tensor_copy(upto[:, :], cst[:, C_UPTO:C_UPTO + P]),
                lambda: nc.vector.tensor_copy(iota[:, :], cst[:, C_IOTA:C_IOTA + P]),
                lambda: nc.vector.tensor_copy(blocks[:, :], cst[:, C_BLOCK:C_BLOCK + BLOCKS]),
                lambda: nc.vector.tensor_scalar(iota1[:, :], cst[:, C_IOTA:C_IOTA + P], 1.0, None, ALU.add),
                lambda: nc.vector.tensor_scalar(pairi[:, :], srci[:, :], 8, None, ALU.arith_shift_right),
                lambda: nc.vector.tensor_scalar(parity[:, :], srci[:, :], 1, None, ALU.bitwise_and),
                lambda: nc.vector.tensor_scalar(place[:, :], srci[:, :], 1, None, ALU.arith_shift_right),
                lambda: nc.vector.memset(ones[:, :].bitcast(f32), 1.0),
                lambda: nc.vector.memset(bias1[:, :].bitcast(f32), 0.0),
            ]
            for f in steps:
                f().then_inc(idx_ready, 1)
            dve.wait_ge(idx_ready, len(steps))
            nc.vector.tensor_copy(pairf[:, :], pairi[:, :]).then_inc(idx_ready, 1)
            nc.vector.tensor_copy(parityf[:, :], parity[:, :]).then_inc(idx_ready, 1)
            nc.vector.tensor_scalar(loci[:, :], place[:, :], 127, None, ALU.bitwise_and).then_inc(idx_ready, 1)
            dve.wait_ge(idx_ready, len(steps) + 3)
            nc.vector.scalar_tensor_tensor(out=blkf[:, :], in0=pairf[:, :], scalar=2.0, in1=parityf[:, :],
                                           op0=ALU.mult, op1=ALU.add).then_inc(idx_ready, 1)
            nc.vector.tensor_scalar(locf[:, :], loci[:, :], 1.0, None, ALU.add).then_inc(idx_ready, 1)
            N_IDX = len(steps) + 5
            dve.wait_ge(w1_hi, 1)
            nc.vector.tensor_tensor(w1l[:, :, :], stage[:, :, :], w1h[:, :, :].bitcast(f32), ALU.subtract)\
                .then_inc(w_split, 1)
            dve.wait_ge(b1_mm, 1)
            nc.vector.tensor_copy(bias1h[0:2, :], pe_m[0:2, 0, 0:D]).then_inc(b1_hi, 1)
            dve.wait_ge(b1_hi, 1)
            nc.vector.scalar_tensor_tensor(out=bias1[0:2, :], in0=bias1h[0:2, :].bitcast(f32),
                                           scalar=cst[0:2, C_LO1:C_LO1 + 1], in1=pe_m[0:2, 0, 0:D],
                                           op0=ALU.mult, op1=ALU.add).then_inc(w_split, 1)

            dve.wait_ge(cst_ready, 2)
            dve.wait_ge(idx_ready, N_IDX)

            def edge_lo(t, u):
                dve.wait_ge(e_hi, t + 1)
                need(dve, e_mm, t - 1)
                nc.vector.tensor_tensor(el[:, u % 2, :], pe_t[:, u % 2, :], eh[:, u % 2, :].bitcast(f32),
                                        ALU.subtract).then_inc(e_lo, 1)

            def edge_block(t, u):
                need(dve, e_tab, t - 1)
                nc.vector.tensor_scalar(ohb[:, u % 2, :], blocks[:, :], blkf[:, bass.ds(t, 1)], None, ALU.is_equal)\
                    .then_inc(e_oh, 1)

            def edge_local(t, u):
                need(dve, e_stored[u], 16 * uses(t, EU, u))
                nc.vector.tensor_copy(msg[:, u, LOC:LOC + 1], locf[:, bass.ds(t, 1)]).then_inc(e_loc, 1)

            def edge_message_lo(t, u):
                dve.wait_ge(e_mh, t + 1)
                nc.vector.tensor_tensor(msg[:, u, HALF:HALF + D], sil[:, u % 2, :], msg[:, u, 0:D].bitcast(f32),
                                        ALU.subtract).then_inc(e_ml, 1)

            def edge_rank(t, u):
                dve.wait_ge(e_cum, t + 1)
                nc.vector.scalar_tensor_tensor(out=picked[:, :], in0=p_cum[:, 0:BLOCKS], scalar=1.0,
                                               in1=ohb[:, u % 2, :], op0=ALU.mult, op1=ALU.mult,
                                               accum_out=rank[:, u % 2:u % 2 + 1]).then_inc(e_rank, 1)

            def edge_slot(t, u):
                dve.wait_ge(e_rank, t + 1)
                need(dve, e_tab, t - 1)
                r = rank[:, u % 2:u % 2 + 1]
                nc.vector.tensor_scalar(oha[:, u % 2, :], iota[:, :], r, cst[:, bass.ds(C_CODE + t, 1)],
                                        ALU.is_equal, ALU.mult).then_inc(e_one, 1)
                nc.vector.tensor_copy(ranks[:, bass.ds(t, 1)], r).then_inc(e_one, 1)

            edge_lo(0, 0)
            edge_block(0, 0)

            def edge_turn(t0, more=True):
                for u in range(EU):
                    t = t0 + u
                    edge_rank(t, u)
                    if not isinstance(t0, int) or t > 0:
                        edge_message_lo(t0 + (u - 1), (u - 1) % EU)
                    if more or u + 1 < EU:
                        edge_block(t0 + (u + 1), (u + 1) % EU)
                    edge_slot(t, u)
                    if more or u + 1 < EU:
                        edge_lo(t0 + (u + 1), (u + 1) % EU)
                    edge_local(t, u)

            edge_turn(0)
            with dve.Fori(1, TILES // EU - 1) as g:
                edge_turn(g * EU)
            edge_turn(TILES - EU, more=False)
            edge_message_lo(TILES - 1, (TILES - 1) % EU)

            def make_table(step, n, done):
                code = p_tab[:, 0:BLOCKS].bitcast(i32)
                high, low, place_ = (slot_bits[:, k, :] for k in range(3))
                empty, first, row, summed = (slot_parts[:, k, :] for k in range(4))
                nc.vector.tensor_scalar(slot_used[:, :], p_tab[:, 0:BLOCKS], 0.0, None, ALU.is_gt).then_inc(step, 1)
                nc.vector.tensor_scalar(empty, p_tab[:, 0:BLOCKS], 0.0, EMPTY, ALU.is_equal, ALU.mult).then_inc(step, 1)
                nc.vector.tensor_scalar(high, code, 23, None, ALU.arith_shift_right).then_inc(step, 1)
                nc.vector.tensor_scalar(low, code, 13, T_LOW - 1, ALU.arith_shift_right, ALU.bitwise_and)\
                    .then_inc(step, 1)
                nc.vector.tensor_scalar(place_, code, 16, P - 1, ALU.arith_shift_right, ALU.bitwise_and)\
                    .then_inc(step, 1)
                dve.wait_ge(step, n + 5)
                nc.vector.tensor_scalar(first, high, float(-CODE_EXP), float(T_LOW * P), ALU.add, ALU.mult)\
                    .then_inc(step, 1)
                nc.vector.scalar_tensor_tensor(out=row, in0=low, scalar=float(P), in1=place_,
                                               op0=ALU.mult, op1=ALU.add).then_inc(step, 1)
                dve.wait_ge(step, n + 7)
                nc.vector.tensor_tensor(summed, first, row, ALU.add).then_inc(step, 1)
                dve.wait_ge(step, n + 8)
                nc.vector.tensor_tensor(slot_row[:, :], summed, empty, ALU.add).then_inc(done, 1)

            TABLE_STEPS = 8
            dve.wait_ge(e_one, 2 * TILES)
            nc.vector.reduce_max(top[:, :], ranks[:, :], axis=mybir.AxisListType.X).then_inc(lv_top, 1)
            dve.wait_ge(e_tab, TILES)
            make_table(t_step, 0, tab_ready)
            dve.wait_ge(lv_row, 1)
            nc.vector.reduce_max(levf[:, :], p_cum[0:1, 0:P], axis=mybir.AxisListType.X).then_inc(lv_top, 1)
            dve.wait_ge(lv_top, 2)
            nc.vector.tensor_scalar(levi[:, :], levf[:, :], float(P), None, ALU.add).then_inc(lv_top, 1)
            dve.wait_ge(lv_top, 3)
            nc.vector.tensor_scalar(levels[:, :], levi[:, :], 7, None, ALU.arith_shift_right).then_inc(lv_ready, 1)

            dve.wait_ge(w_hi, 1)
            nc.vector.tensor_tensor(wxl[:, :, :], whh[:, :, :], wxh[:, :, :].bitcast(f32), ALU.subtract)\
                .then_inc(setup_cp, 1)
            for k in range(KC):
                for c, (n0, n1) in enumerate(((0, 2 * D), (2 * D, 3 * D))):
                    dve.wait_ge(w_hi, 2 + 2 * k + c)
                    nc.vector.tensor_tensor(wsl[:, k, n0:n1], p_wc[k][:, c, 0:n1 - n0], wsh[:, k, n0:n1].bitcast(f32),
                                            ALU.subtract).then_inc(setup_cp, 1)
            for c in range(2):
                dve.wait_ge(w_hi, 2 + 2 * KC + c)
                nc.vector.scalar_tensor_tensor(
                    out=bias[0:BROWS, c * 2 * D:(c + 1) * 2 * D], in0=biash[:, c * 2 * D:(c + 1) * 2 * D].bitcast(f32),
                    scalar=cst[0:BROWS, C_LO4:C_LO4 + 1], in1=p_bias[0:BROWS, c, :],
                    op0=ALU.mult, op1=ALU.add).then_inc(setup_cp, 1)

            dve.wait_ge(lv_ready, 1)
            n_levels = dve.value_load(levels[0:1, 0:1], min_val=1, max_val=TILES)
            with dve.If(n_levels > 1):
                nc.vector.memset(put[:, :].bitcast(f32), 0.0).then_inc(v_zero, 1)
                dve.wait_ge(v_zero, 1)
                nc.vector.tensor_copy(put[:, LOC:LOC + 1], cst[:, C_PART:C_PART + 1]).then_inc(v_zero, 1)
                with dve.Fori(0, n_levels) as lv:
                    with dve.Fori(0, TILES) as t:
                        dve.wait_ge(v_tab, lv * TILES + t + 1)
                        nc.vector.tensor_scalar(ohb[:, 0, :], blocks[:, :], blkf[:, bass.ds(t, 1)], None,
                                                ALU.is_equal).then_inc(v_oh, 1)
                        nc.vector.tensor_scalar(oha[:, 0, :], iota[:, :], ranks[:, bass.ds(t, 1)],
                                                cst[:, bass.ds(C_CODE + t, 1)], ALU.is_equal, ALU.mult)\
                            .then_inc(v_oh, 1)
                    dve.wait_ge(v_tab, lv * TILES + TILES + 1)
                    make_table(v_step, lv * (TABLE_STEPS + 1), v_rows)
                    nc.vector.tensor_scalar(ranks[:, :], ranks[:, :], float(-P), None, ALU.add).then_inc(v_step, 1)
                    need_apart(dve, dve_passed, v_step, (lv + 1) * (TABLE_STEPS + 1))
                    with dve.Fori(0, BLOCKS) as b:
                        n = lv * BLOCKS + b
                        dve.wait_ge(v_got, n * 16 + 16)
                        nc.vector.tensor_scalar(oh[:, 0, 0, :], iota1[:, :], mg[:, 0, 0, LOC:LOC + 1].bitcast(f32),
                                                slot_used[:, bass.ds(b, 1)], ALU.is_equal, ALU.mult)\
                            .then_inc(v_one, 1)
                        dve.wait_ge(v_sum, n + 2)
                        dve.wait_ge(v_prev, n * 16 + 16)
                        nc.vector.tensor_tensor(total[:, 0, :], pn_s[:, 0, 0:SUMMED],
                                                before[:, 0:SUMMED].bitcast(f32), ALU.add).then_inc(v_acc, 1)
                        dve.wait_ge(v_acc, n * 3 + 1)
                        nc.vector.tensor_tensor(total[:, 1, :], total[:, 0, :],
                                                before[:, HALF:HALF + SUMMED].bitcast(f32), ALU.add)\
                            .then_inc(v_acc, 1)
                        dve.wait_ge(v_acc, n * 3 + 2)
                        nc.vector.tensor_copy(put[:, 0:SUMMED], total[:, 1, :]).then_inc(v_acc, 1)
                        dve.wait_ge(v_acc, n * 3 + 3)
                        nc.vector.tensor_tensor(put[:, HALF:HALF + SUMMED], total[:, 1, :],
                                                put[:, 0:SUMMED].bitcast(f32), ALU.subtract).then_inc(v_add, 1)
                nc.vector.memset(slot_used[:, :], 1.0).then_inc(tab_ready, 1)
                dve.wait_ge(tab_ready, 2)

            def one_hot(q, u):
                need(dve, S["n_seg"], q - QU + 1)
                for h in range(2):
                    dve.wait_ge(got_m[2 * u + h], 16 * (uses(q, QU, u) + 1))
                    last = nc.vector.tensor_scalar(oh[:, u, h, :], iota1[:, :],
                                                   mg[:, u, h, LOC:LOC + 1].bitcast(f32),
                                                   slot_used[:, bass.ds(q * 2 + h, 1)], ALU.is_equal, ALU.mult)
                last.then_inc(S["n_oh"], 1)

            def gated_h(q, u):
                dve.wait_ge(S["n_rz"], q + 1)
                nc.vector.tensor_tensor(rhn[:, u % 2, :, :], rz[:, u, :, 0:D], pn_n[:, :, 0:D], ALU.mult)\
                    .then_inc(S["n_rhn"], 1)

            def n_input(q, u):
                dve.wait_ge(S["n_rhn"], q + 1)
                need(dve, S["n_tanh"], q - 1)
                nc.vector.tensor_tensor(npre[:, u % 2, :].rearrange("p (h d) -> p h d", h=2), rhn[:, u % 2, :, :],
                                        pn_n[:, :, D:2 * D], ALU.add).then_inc(S["n_npre"], 1)

            def s_lo(q, u):
                dve.wait_ge(S["n_sh"], q + 1)
                nc.vector.tensor_tensor(sl[:, u % 2, :], pn_t[:, u % 2, :], sh[:, u % 2, :].bitcast(f32),
                                        ALU.subtract).then_inc(S["n_sl"], 1)

            def count_eps(q, u):
                dve.wait_ge(S["n_has"], q + 1)
                nc.vector.tensor_scalar(cnt_eps[:, u, :], pn_s[:, :, CNT], EPS_CNT, None, ALU.add)\
                    .then_inc(S["n_ce"], 1)

            def count_inv(q, u):
                dve.wait_ge(S["n_ce"], q + 1)
                need(dve, S["n_mean"], q - QU + 1)
                nc.vector.reciprocal(rcount[:, u, :], cnt_eps[:, u, :]).then_inc(S["n_rc"], 1)

            def z_diff(q, u):
                dve.wait_ge(S["n_diff"], q + 1)
                nc.vector.tensor_tensor(zd[:, u % 2, :].rearrange("p (h d) -> p h d", h=2), rz[:, u, :, D:2 * D],
                                        diff[:, u, :].rearrange("p (h d) -> p h d", h=2), ALU.mult)\
                    .then_inc(S["n_zd"], 1)

            def x_new(q, u):
                dve.wait_ge(S["n_zd"], q + 1)
                nc.vector.tensor_tensor(xn[:, u % 2, :], zd[:, u % 2, :], nt[:, u, :], ALU.add)\
                    .then_inc(S["n_xn"], 1)

            def stats(q, u, tile, before, st, done):
                dve.wait_ge(before, q + 1)
                for h in range(2):
                    last = nc.vector.bn_stats(st[:, u, h, :], tile[:, h * D:(h + 1) * D])
                last.then_inc(done, 1)

            def aggregate(q, u, before, st, ag, done):
                need_apart(dve, dve_passed, before, q + 1)
                for h in range(2):
                    last = nc.vector.bn_aggr(ag[:, u, h, :], st[:, u, h, :])
                last.then_inc(done, 1)

            def var_eps(q, u, before, ag, ve, done):
                dve.wait_ge(before, q + 1)
                nc.vector.tensor_scalar(ve[:, u, :], ag[:, u, :, 1], EPS_LN, None, ALU.add).then_inc(done, 1)

            def scale_gamma(q, u):
                dve.wait_ge(S["n_a1"], q + 1)
                for h in range(2):
                    last = nc.vector.scalar_tensor_tensor(
                        out=tg[:, u % 2, h * D:(h + 1) * D], in0=xn[:, u % 2, h * D:(h + 1) * D],
                        scalar=ag1[:, u, h, 0:1], in1=gammab[:, :], op0=ALU.subtract, op1=ALU.mult)
                last.then_inc(S["n_tg"], 1)

            def residual(q, u):
                dve.wait_ge(S["n_tg"], q + 1)
                dve.wait_ge(S["n_r1"], q + 1)
                dve.wait_ge(S["n_xb"], q + 1)
                need(dve, S["n_y"], q - QU + 1)
                for h in range(2):
                    last = nc.vector.scalar_tensor_tensor(
                        out=uu[:, u, h * D:(h + 1) * D], in0=tg[:, u % 2, h * D:(h + 1) * D],
                        scalar=rs1[:, u, h:h + 1], in1=xb[:, u, h * D:(h + 1) * D], op0=ALU.mult, op1=ALU.add)
                last.then_inc(S["n_u"], 1)

            def minus_mean(q, u):
                dve.wait_ge(S["n_r2"], q + 1)
                nc.vector.scalar_tensor_tensor(out=nmr[:, u, :], in0=ag2[:, u, :, 0], scalar=-1.0, in1=rs2[:, u, :],
                                               op0=ALU.mult, op1=ALU.mult).then_inc(S["n_nmr"], 1)

            def stats1(q, u):
                stats(q, u, xn[:, u % 2, :], S["n_xn"], st1, S["n_s1"])

            def stats2(q, u):
                stats(q, u, uu[:, u, :], S["n_u"], st2, S["n_s2"])

            def aggregate1(q, u):
                aggregate(q, u, S["n_s1"], st1, ag1, S["n_a1"])

            def aggregate2(q, u):
                aggregate(q, u, S["n_s2"], st2, ag2, S["n_a2"])

            def var_eps1(q, u):
                var_eps(q, u, S["n_a1"], ag1, ve1, S["n_v1"])

            def var_eps2(q, u):
                var_eps(q, u, S["n_a2"], ag2, ve2, S["n_v2"])

            edges_done(dve)
            node_turns(dve, ((gated_h, -1), (s_lo, 1), (n_input, -1), (z_diff, -2), (count_eps, 2), (residual, -3),
                             (count_inv, 2), (x_new, -2), (minus_mean, -4), (stats2, -3), (stats1, -2),
                             (aggregate2, -3), (one_hot, 3), (aggregate1, -2), (var_eps2, -3), (var_eps1, -2),
                             (scale_gamma, -2)), first=-3, last=4)

        @block.tensor
        def _(pe):
            def mm(out_, lhsT, rhs, start, stop, skip=False):
                return nc.tensor.matmul(out_, lhsT, rhs, start=start, stop=stop, skip_group_check=skip)

            pe.wait_ge(ld_c, 16)
            pe.wait_ge(ld_w1, 32)
            mm(pe_m[0:2, 0, 0:D], cst[0:1, C_SEL + 32:C_SEL + 34], brow[:, 6 * D:7 * D], True, True).then_inc(b1_mm, 1)

            def edge_transpose(t, u):
                pe.wait_ge(got_src[u], 16 * (uses(t, EU, u) + 1))
                pe.wait_ge(got_dst[u], 16 * (uses(t, EU, u) + 1))
                need(pe, e_lo, t - 1)
                for c in range(2 * KC):
                    tile = (xsrc if c < KC else xdst)[:, u, (c % KC) * P:(c % KC + 1) * P]
                    last = nc.tensor.transpose(pe_t[:, u % 2, c * P:(c + 1) * P], tile, ident)
                last.then_inc(e_xt, 1)

            def edge_earlier(t, u, first=False):
                pe.wait_ge(e_oh, t + 1)
                mm(p_cum[:, 0:BLOCKS], lower[:, :], ohb[:, u % 2, :], first, True, True).then_inc(e_cum, 1)

            def edge_products(t, u):
                pe.wait_ge(e_lo, t + 1)
                need(pe, e_msg, t - 1)
                o = pe_m[:, u % 2, 0:D]
                for c in range(2 * KC):
                    h, l = (a[:, u % 2, c * P:(c + 1) * P] for a in (eh, el))
                    mm(o, h, w1h[:, c, :], c == 0, False)
                    mm(o, h, w1l[:, c, :], False, False)
                    mm(o, l, w1h[:, c, :], False, False)
                mm(o, ones[:, :], bias1[:, :], False, True).then_inc(e_mm, 1)

            def edge_table(t, u, first=False):
                pe.wait_ge(e_rank, t + 1)
                mm(p_cum[:, 0:BLOCKS], upto[:, :], ohb[:, u % 2, :], False, True, True)
                pe.wait_ge(e_one, 2 * t + 1)
                mm(p_tab[:, 0:BLOCKS], oha[:, u % 2, :], ohb[:, u % 2, :], first, True, True).then_inc(e_tab, 1)

            edge_transpose(0, 0)
            pe.wait_ge(w_split, 2)
            pe.wait_ge(idx_ready, 10)

            def edge_turn(t0, more=True, first=False):
                for u in range(EU):
                    t = t0 + u
                    edge_earlier(t, u, first and u == 0)
                    if more or u + 1 < EU:
                        edge_transpose(t0 + (u + 1), (u + 1) % EU)
                    edge_products(t, u)
                    edge_table(t, u, first and u == 0)

            edge_turn(0, first=True)
            with pe.Fori(1, TILES // EU - 1) as g:
                edge_turn(g * EU)
            edge_turn(TILES - EU, more=False)

            def segment_products(bank, one_hots, rows):
                mm(bank[:, 0:SUMMED], one_hots, rows[:, 0:SUMMED], True, False)
                return mm(bank[:, 0:SUMMED], one_hots, rows[:, HALF:HALF + SUMMED], False, True)

            pe.wait_ge(lv_top, 1)
            mm(p_cum[0:1, 0:P], top[:, :], ident, True, True).then_inc(lv_row, 1)

            pe.wait_ge(ld_w, 16 * W_LOADS)
            pe.wait_ge(node_ready, 5)
            pe.wait_ge(e_msg, TILES)
            pe.wait_ge(e_lo, TILES)
            for i in range(KC):
                for c, (n0, n1) in enumerate(((0, 2 * D), (2 * D, 3 * D))):
                    for o in range(KC):
                        last = mm(p_wc[i][:, c, 0:n1 - n0], w2s[:, o, i * P:(i + 1) * P], wih[:, o, n0:n1],
                                  o == 0, o == KC - 1)
                last.then_inc(setup_mm, 1)
            sel = cst[0:1, C_SEL:C_SEL + BROWS]
            for o in range(KC):
                mm(p_bias[0:BROWS, 0, :], b2s[:, o, :], wih[:, o, 0:2 * D], o == 0, False)
            mm(p_bias[0:BROWS, 0, :], sel, brow[:, 0:2 * D], False, False)
            mm(p_bias[0:BROWS, 0, :], sel, brow[:, 3 * D:5 * D], False, True)
            mm(p_bias[0:BROWS, 1, 0:D], sel, brow[:, 5 * D:6 * D], True, True)
            for o in range(KC):
                mm(p_bias[0:BROWS, 1, D:2 * D], b2s[:, o, :], wih[:, o, 2 * D:3 * D], o == 0, False)
            mm(p_bias[0:BROWS, 1, D:2 * D], sel, brow[:, 2 * D:3 * D], False, True).then_inc(setup_mm, 1)
            pe.wait_ge(setup_cp, WC_PARTS + 1)

            pe.wait_ge(lv_ready, 1)
            n_levels = pe.value_load(levels[0:1, 0:1], min_val=1, max_val=TILES)
            with pe.If(n_levels > 1):
                pe.sem_inc(v_tab)
                pe.sem_inc(v_sum)
                with pe.Fori(0, n_levels) as lv:
                    def level_tile(t, first):
                        pe.wait_ge(v_oh, (lv * TILES + t) * 2 + 2)
                        mm(p_tab[:, 0:BLOCKS], oha[:, 0, :], ohb[:, 0, :], first, True, True).then_inc(v_tab, 1)
                    level_tile(0, True)
                    with pe.Fori(1, TILES) as t:
                        level_tile(t, False)
                    with pe.Fori(0, BLOCKS) as b:
                        pe.wait_ge(v_one, lv * BLOCKS + b + 1)
                        segment_products(pn_s[:, 0, :], oh[:, 0, 0, :], mg[:, 0, 0, :]).then_inc(v_sum, 1)

            def segment_sum(q, u):
                pe.wait_ge(S["n_oh"], q + 1)
                need(pe, S["n_mean"], q)
                for h in range(2):
                    one_hots, rows = oh[:, u, h, :], mg[:, u, h, :]
                    segment_products(pn_s[:, h, :], one_hots, rows)
                    last = mm(pn_s[:, h, 384:384 + P], rows[:, CNT:CNT + P], one_hots, True, True)
                last.then_inc(S["n_seg"], 1)

            def s_transpose(q, u):
                pe.wait_ge(S["n_mean"], q + 1)
                need(pe, S["n_sl"], q - 1)
                for h in range(2):
                    for c in range(KC):
                        last = nc.tensor.transpose(pn_t[:, u % 2, (2 * h + c) * P:(2 * h + c + 1) * P],
                                                   mean[:, u % 2, h, c * P:(c + 1) * P], ident)
                last.then_inc(S["n_st"], 1)

            def products(q, u):
                pe.wait_ge(S["n_xl"], q + 1)
                pe.wait_ge(S["n_sl"], q + 1)
                pe.wait_ge(S["n_has"], q + 1)

                def part(o, side, h, n0, n1, first, last=False):
                    hi, lo, whi, wlo = side
                    for c in range(KC):
                        a, b = (t[:, (2 * h + c) * P:(2 * h + c + 1) * P] for t in (hi, lo))
                        mm(o, a, whi[:, c, n0:n1], first and c == 0, False)
                        mm(o, a, wlo[:, c, n0:n1], False, False)
                        mm(o, b, whi[:, c, n0:n1], False, last and c == KC - 1)

                x_ = xh[:, u, :], xl[:, u, :], wxh, wxl
                s_ = sh[:, u % 2, :], sl[:, u % 2, :], wsh, wsl
                for h in range(2):
                    has = hasrow[:, u, h, :]
                    o_rz, o_h, o_i = pn_rz[:, h, :], pn_n[:, h, 0:D], pn_n[:, h, D:2 * D]
                    need(pe, S["n_rz0" if h == 0 else "n_rz"], q)
                    part(o_rz, x_, h, 0, 2 * D, True)
                    part(o_rz, s_, h, 0, 2 * D, False)
                    mm(o_rz, has, bias[:, 0:2 * D], False, True)
                    if h == 0:
                        need(pe, S["n_npre"], q)
                    part(o_h, x_, h, 2 * D, 3 * D, True)
                    mm(o_h, has, bias[:, 2 * D:3 * D], False, True)
                    part(o_i, s_, h, 2 * D, 3 * D, True)
                    mm(o_i, has, bias[:, 3 * D:4 * D], False, True).then_inc(S["n_mm0" if h == 0 else "n_mm"], 1)

            node_turns(pe, ((s_transpose, 1), (segment_sum, 2), (products, 0)), first=-2, last=0)


def kernel(x, src, dst, L0_gnn_W1, L0_gnn_b1, L0_gnn_W2, L0_gnn_b2, L0_gnn_w_ih, L0_gnn_w_hh,
           L0_gnn_b_ih, L0_gnn_b_hh, L0_gnn_gamma, L0_gnn_beta):
    import concourse.bacc as bacc
    from concourse.bass_utils import run_bass_kernel_spmd

    def arr(a):
        return np.ascontiguousarray(np.asarray(a))
    x, src, dst = arr(x), arr(src), arr(dst)
    xp = np.zeros((NODES_PAD, D), x.dtype)
    xp[:NODES] = x
    pad = EDGES_PAD - EDGES
    srcp = np.concatenate([src, (NODES_PAD - 1 - 2 * np.arange(pad)).astype(src.dtype)])
    xt = xp.reshape(PAIRS, P, 2, KC, P).transpose(0, 4, 2, 3, 1).reshape(PAIRS * P, 2 * D)
    dstp = np.concatenate([dst, np.zeros(pad, dst.dtype)])
    ins = {
        "x": xp, "xt": arr(xt), "src": srcp, "dst": dstp, "w1t": arr(arr(L0_gnn_W1).T), "b1": arr(L0_gnn_b1),
        "w2": arr(L0_gnn_W2), "b2": arr(L0_gnn_b2), "wiht": arr(arr(L0_gnn_w_ih).T),
        "whht": arr(arr(L0_gnn_w_hh).T), "bih": arr(L0_gnn_b_ih), "bhh": arr(L0_gnn_b_hh),
        "gamma": arr(L0_gnn_gamma), "beta": arr(L0_gnn_beta), "consts": constants(),
    }
    nc = bacc.Bacc("TRN2", target_bir_lowering=False, num_devices=1)
    arrays, args = {}, []
    for name, a in ins.items():
        arrays[f"in_{name}"] = a
        args.append(nc.dram_tensor(f"in_{name}", a.shape, mybir.dt.from_np(a.dtype), kind="ExternalInput").ap())
    args.append(nc.dram_tensor("out_y", (NODES_PAD, D), mybir.dt.float32, kind="ExternalOutput").ap())
    gnn_layer(nc, *args)
    r = run_bass_kernel_spmd(nc, [arrays], core_ids=[0])
    return r.results[0]["out_y"][:NODES]
```

```python
from contextlib import ExitStack

import numpy as np

import concourse.bass as bass
from concourse import mybir

P = 128
D = 256
KC = D // P
NODES = 50000
EDGES = 25000
BLOCKS = 392
PAIRS = BLOCKS // 2
NODES_PAD = BLOCKS * P
TILES = 196
EDGES_PAD = TILES * P
EU = 4
QU = 4
TURNS = PAIRS // QU
CNT = D
LOC = D + 2
SUMMED = D + 2
HALF = D + 4
ROW = 2 * HALF
EMPTY = float(1 << 20)
T_LOW = 8
CODE_EXP = 127 + 10 - 24
EPS_LN = 1e-5
EPS_CNT = 1e-8

C_IDENT, C_LOWER, C_UPTO, C_IOTA = 0, P, 2 * P, 3 * P
C_BLOCK = 4 * P
C_CODE = C_BLOCK + BLOCKS
C_PART = C_CODE + TILES
C_ALL = C_PART + 1


def constants():
    c = np.zeros((P, C_ALL), np.float32)
    i = np.arange(P)
    c[:, C_IDENT:C_IDENT + P] = np.eye(P)
    c[:, C_LOWER:C_LOWER + P] = i[:, None] < i[None, :]
    c[:, C_UPTO:C_UPTO + P] = i[:, None] >= i[None, :]
    c[:, C_IOTA:C_IOTA + P] = i[None, :]
    c[:, C_BLOCK:C_BLOCK + BLOCKS] = np.arange(BLOCKS)[None, :]
    t = np.arange(TILES)[None, :]
    c[:, C_CODE:C_CODE + TILES] = (1024 + i[:, None] * T_LOW + t % T_LOW) * 2.0 ** (t // T_LOW - 24)
    c[:, C_PART] = i + 1
    return c


def gnn_layer(nc, x, xt, src, dst, w1t, b1, w2, b2, wiht, whht, bih, bhh, gamma, beta, consts, out):
    f32, f32r, bf16, i32 = mybir.dt.float32, mybir.dt.float32r, mybir.dt.bfloat16, mybir.dt.int32
    fp16 = mybir.dt.float16
    ACT, ALU = mybir.ActivationFunctionType, mybir.AluOpType
    ctx = ExitStack()
    with ctx:
        def sb(name, shape, dt=f32, until=ctx):
            return until.enter_context(nc.sbuf_tensor(name, shape, dt))

        def sem(name):
            return ctx.enter_context(nc.semaphore(name))

        def sems(name, n):
            return [sem(f"{name}{i}") for i in range(n)]

        messages = nc.dram_tensor("messages", [EDGES_PAD, ROW], f32, kind="Internal").ap()
        sums = nc.dram_tensor("sums", [NODES_PAD, ROW], f32, kind="Internal").ap()

        cst = sb("cst", [P, C_ALL])
        ident = cst[:, C_IDENT:C_IDENT + P]
        lower = sb("lower", [P, P], fp16)
        upto = sb("upto", [P, P], fp16)
        iota = sb("iota", [P, P], fp16)
        blocks = sb("blocks", [P, BLOCKS], fp16)
        iota1 = sb("iota1", [P, P])
        srci = sb("srci", [P, TILES], i32)
        dsti = sb("dsti", [P, TILES], i32)
        blkf = sb("blkf", [P, TILES])
        locf = sb("locf", [P, TILES])
        ranks = sb("ranks", [P, TILES])
        slot_row = sb("slot_row", [P, BLOCKS], i32)
        slot_used = sb("slot_used", [P, BLOCKS])
        wxh, wxl = sb("wxh", [P, KC, 3 * D], f32r), sb("wxl", [P, KC, 3 * D], f32r)
        wsh, wsl = sb("wsh", [P, KC, 3 * D], f32r), sb("wsl", [P, KC, 3 * D], f32r)
        rz_b, rz_c, in_c = sb("rz_b", [P, 2 * D]), sb("rz_c", [P, 2 * D]), sb("in_c", [P, D])
        hn_b, in_b = sb("hn_b", [P, 2, D]), sb("in_b", [P, D])
        ones = sb("ones", [P, P], f32r)
        gammab, betab = sb("gammab", [P, D]), sb("betab", [P, 2 * D])

        XE = 4
        src_now, dst_now = sb("src_now", [P, 2, EU], i32), sb("dst_now", [P, 2, EU], i32)
        rows_now = sb("rows_now", [P, 2 * QU], i32)
        msg = sb("msg", [P, EU, ROW], f32r)
        ohb = sb("ohb", [P, 2, BLOCKS], fp16)
        rank = sb("rank", [P, 2])
        oha = sb("oha", [P, 2, P], fp16)

        mg = sb("mg", [P, QU, 2, ROW], f32r)
        oh = sb("oh", [P, QU, 2, P], f32r)
        has = sb("has", [P, QU, 2])
        halves = sb("halves", [P, 2])

        top, levf, levi = sb("top", [P, 1]), sb("levf", [1, 1]), sb("levi", [1, 1], i32)
        levels = sb("levels", [1, 1], i32)

        early = ExitStack()
        before, total = sb("before", [P, ROW], f32r, until=early), sb("total", [P, 2, SUMMED], until=early)
        put = sb("put", [P, ROW], f32r, until=early)
        slot_bits, slot_parts = sb("slot_bits", [P, 3, BLOCKS], i32, until=early), sb("slot_parts", [P, 4, BLOCKS], until=early)
        parity, place, pairi, loci = (sb(n, [P, TILES], i32, until=early) for n in ("parity", "place", "pairi", "loci"))
        pairf, parityf = sb("pairf", [P, TILES], until=early), sb("parityf", [P, TILES], until=early)
        w1h, w1l = (sb(n, [P, 2 * KC, D], f32r, until=early) for n in ("w1h", "w1l"))
        stage = sb("stage", [P, 2 * KC, D], until=early)
        b1_all = sb("b1_all", [P, D], until=early)
        xsrc, xdst = (sb(n, [P, XE, D], until=early) for n in ("xsrc", "xdst"))
        eh, el = (sb(n, [P, 2, 2 * KC * P], f32r, until=early) for n in ("eh", "el"))
        sil = sb("sil", [P, 2, D], until=early)
        w2s, b2s = sb("w2s", [P, KC, D], until=early), sb("b2s", [P, KC], until=early)
        b2b = sb("b2b", [P, KC, P], until=early)
        brow = sb("brow", [1, 3 * D + 3 * D + D], until=early)
        picked = sb("picked", [P, BLOCKS], fp16, until=early)
        wih, whh = (sb(n, [P, KC, 3 * D], until=early) for n in ("wih", "whh"))
        early.close()

        xs, xts = sb("xs", [P, QU, 2 * D]), sb("xts", [P, QU, 2 * D])
        xh, xl = sb("xh", [P, QU, 2 * D], f32r), sb("xl", [P, QU, 2 * D], f32r)
        mean = sb("mean", [P, 2, 2, D])
        st = sb("st", [P, 2, 2 * D])
        sh, sl = sb("sh", [P, 2, 2 * D], f32r), sb("sl", [P, 2, 2 * D], f32r)
        xb = sb("xb", [P, QU, 2 * D])
        cnt_eps, rcount = sb("cnt_eps", [P, QU, 2]), sb("rcount", [P, QU, 2])
        rz = sb("rz", [P, QU, 2, 2 * D])
        rhn, npre = sb("rhn", [P, 2, 2, D]), sb("npre", [P, 2, 2 * D])
        nt, diff = sb("nt", [P, QU, 2 * D]), sb("diff", [P, QU, 2 * D])
        zd, xn = sb("zd", [P, 2, 2 * D]), sb("xn", [P, 2, 2 * D])
        st1, ag1 = sb("st1", [P, QU, 2, 6]), sb("ag1", [P, QU, 2, 2])
        st2, ag2 = sb("st2", [P, QU, 2, 6]), sb("ag2", [P, QU, 2, 2])
        ve1, ve2, rs1, rs2, nmr = (sb(n, [P, QU, 2]) for n in ("ve1", "ve2", "rs1", "rs2", "nmr"))
        tg, uu, yy = sb("tg", [P, 2, 2 * D]), sb("uu", [P, QU, 2 * D]), sb("yy", [P, QU, 2 * D])

        pairs_of_banks = [ctx.enter_context(nc.psum_tensor(f"banks{i}", [P, 2, 512], f32)) for i in range(4)]
        pe_t, pe_m = pairs_of_banks[0], pairs_of_banks[1]
        p_cum, p_tab = pairs_of_banks[2][:, 0, :], pairs_of_banks[2][:, 1, :]
        p_wc, p_rzb, p_nb = pairs_of_banks[0:2], pairs_of_banks[3], pairs_of_banks[2]
        pn_t, pn_s, pn_rz, pn_n = pairs_of_banks

        ld_w1, ld_w = sem("ld_w1"), sem("ld_w")
        ld_e, ld_c = sem("ld_e"), sem("ld_c")
        cst_ready, w_split, setup_mm, setup_cp, idx_ready = (
            sem("cst_ready"), sem("w_split"), sem("setup_mm"), sem("setup_cp"), sem("idx_ready"))
        w1_hi, b1_mm, b1_ready, w_hi = sem("w1_hi"), sem("b1_mm"), sem("b1_ready"), sem("w_hi")
        node_ready, b2_ready, primed = sem("node_ready"), sem("b2_ready"), sem("primed")
        got_src, got_dst, e_stored = sems("got_src", XE), sems("got_dst", XE), sems("e_stored", EU)
        e_xt, e_hi, e_lo, e_mm, e_msg, e_loc = (sem(n) for n in ("e_xt", "e_hi", "e_lo", "e_mm", "e_msg", "e_loc"))
        e_mh, e_ml, e_seed = sem("e_mh"), sem("e_ml"), sem("e_seed")
        e_oh, e_cum, e_rank, e_one, e_tab = (sem(n) for n in ("e_oh", "e_cum", "e_rank", "e_one", "e_tab"))
        idx_now = sem("idx_now")
        pool_passed, dve_passed, sp_passed = sem("pool_passed"), sem("dve_passed"), sem("sp_passed")
        t_step, tab_ready = sem("t_step"), sem("tab_ready")
        lv_top, lv_row, lv_ready = sem("lv_top"), sem("lv_row"), sem("lv_ready")
        v_zero, v_oh, v_tab, v_step, v_rows = (sem(n) for n in ("v_zero", "v_oh", "v_tab", "v_step", "v_rows"))
        v_idx, v_got, v_one, v_sum, v_prev = (sem(n) for n in ("v_idx", "v_got", "v_one", "v_sum", "v_prev"))
        v_acc, v_add, v_put, v_done = (sem(n) for n in ("v_acc", "v_add", "v_put", "v_done"))
        got_x, got_xt, got_m, n_stored = sems("got_x", QU), sems("got_xt", QU), sems("got_m", 2 * QU), sems("n_stored", QU)
        names = ("n_oh n_xh n_xl n_seg n_ce n_rc n_mean n_st n_sh n_has n_sl n_g0 n_g1 n_mm n_sd0 n_sd1 n_si n_sn n_rz0 n_rz n_rhn n_npre n_tanh"
                 " n_diff n_xb n_zd n_xn n_s1 n_a1 n_v1 n_r1 n_tg n_u n_s2 n_a2 n_v2 n_r2 n_nmr n_y").split()
        S = {n: sem(n) for n in names}

        def need(eng, s, value):
            if not isinstance(value, int) or value > 0:
                eng.wait_ge(s, value)

        def need_apart(eng, passed, s, value):
            need(eng, s, value)
            eng.sem_inc(passed)

        def uses(j, slots, u):
            return j // slots if isinstance(j, int) else (j - u) // slots

        def node_turns(eng, parts, first, last):
            def step(q, u):
                for part, lag in parts:
                    if not isinstance(q, int) or 0 <= q + lag < PAIRS:
                        part(q + lag, (u + lag) % QU)

            head = QU * (-(min(lag for _, lag in parts) // QU) + 1)
            tail = PAIRS - QU * -(-max(lag for _, lag in parts) // QU)
            for q in range(first, head):
                step(q, q % QU)
            with eng.Fori(head // QU, tail // QU) as g:
                for u in range(QU):
                    step(g * QU + u, u)
            for q in range(tail, PAIRS + last):
                step(q, q % QU)

        def edges_done(eng):
            eng.wait_ge(e_mm, TILES)
            eng.wait_ge(e_ml, TILES)

        block = ctx.enter_context(nc.Block())
        W_LOADS = 10
        WC_PARTS = 2 * KC + 1

        @block.sync
        def _(sp):
            loads = [(srci[:, :], src.rearrange("(p t) -> p t", p=P)),
                     (dsti[:, :], dst.rearrange("(p t) -> p t", p=P)), (cst[:, :], consts)]
            for (a, b), done in zip(loads, (ld_e, ld_e, ld_c)):
                sp.dma_start(a, b).then_inc(done, 16)
            sp.dma_start(stage[:, :, :], w1t.rearrange("(k p) n -> p k n", p=P)).then_inc(ld_w1, 16)
            sp.dma_start(brow[:, 6 * D:7 * D], b1.rearrange("(a n) -> a n", a=1)).then_inc(ld_w1, 16)
            more = [(wih[:, :, :], wiht.rearrange("(k p) n -> p k n", p=P)),
                    (w2s[:, :, :], w2.rearrange("(k p) n -> p k n", p=P)),
                    (whh[:, :, :], whht.rearrange("(k p) n -> p k n", p=P)),
                    (brow[:, 0:3 * D], bih.rearrange("(a n) -> a n", a=1)),
                    (brow[:, 3 * D:6 * D], bhh.rearrange("(a n) -> a n", a=1)),
                    (gammab[:, :], gamma.rearrange("(a n) -> a n", a=1).to_broadcast([P, D])),
                    (betab[:, 0:D], beta.rearrange("(a n) -> a n", a=1).to_broadcast([P, D])),
                    (betab[:, D:2 * D], beta.rearrange("(a n) -> a n", a=1).to_broadcast([P, D]))]
            for k in range(KC):
                more.append((b2s[:, k:k + 1], b2[k * P:(k + 1) * P].rearrange("(p a) -> p a", a=1)))
            for a, b in more:
                sp.dma_start(a, b).then_inc(ld_w, 16)
            assert len(more) == W_LOADS

            def store_messages(t, u):
                sp.wait_ge(e_ml, t + 1)
                sp.wait_ge(e_loc, t + 1)
                sp.dma_start(messages[bass.ds(t * P, P), :], msg[:, u, :].bitcast(f32)).then_inc(e_stored[u], 16)

            for u in range(EU):
                store_messages(u, u)
            with sp.Fori(1, TILES // EU) as g:
                for u in range(EU):
                    store_messages(g * EU + u, u)

            sp.wait_ge(lv_ready, 1)
            n_levels = sp.value_load(levels[0:1, 0:1], min_val=1, max_val=TILES)
            with sp.If(n_levels > 1):
                sp.wait_ge(v_zero, 2)
                with sp.Fori(0, BLOCKS) as b:
                    sp.dma_start(sums[bass.ds(b * P, P), :], put[:, :].bitcast(f32)).then_inc(v_put, 16)
                    need_apart(sp, sp_passed, v_put, b * 16 + 16)
                with sp.Fori(0, n_levels) as lv:
                    with sp.Fori(0, BLOCKS) as b:
                        n = lv * BLOCKS + b
                        sp.dma_start(before[:, :].bitcast(f32), sums[bass.ds(b * P, P), :]).then_inc(v_prev, 16)
                        need_apart(sp, sp_passed, v_add, n + 1)
                        sp.dma_start(sums[bass.ds(b * P, P), :], put[:, :].bitcast(f32)).then_inc(v_put, 16)
                        need_apart(sp, sp_passed, v_put, n * 16 + 16 * (BLOCKS + 1))
                sp.sem_inc(v_done)

            x_pairs = x.rearrange("(r h) d -> r (h d)", h=2)
            out_pairs = out.rearrange("(r h) d -> r (h d)", h=2)

            def load_x(q, u):
                need(sp, S["n_xl"], q - QU + 1)
                sp.dma_start(xts[:, u, :], xt[bass.ds(q * P, P), :]).then_inc(got_xt[u], 16)
                need(sp, S["n_diff"], q - QU + 1)
                need(sp, S["n_xb"], q - QU + 1)
                sp.dma_start(xs[:, u, :], x_pairs[bass.ds(q * P, P), :]).then_inc(got_x[u], 16)

            def store_y(q, u):
                sp.wait_ge(S["n_y"], q + 1)
                sp.dma_start(out_pairs[bass.ds(q * P, P), :], yy[:, u, :]).then_inc(n_stored[u], 16)

            edges_done(sp)
            sp.wait_ge(tab_ready, 1)
            node_turns(sp, ((load_x, 3), (store_y, -5)), first=-3, last=5)
            for s in range(QU):
                sp.wait_ge(n_stored[s], 16 * TURNS)

        def gather(dst_tile, table, rows, done, bound=None):
            nc.gpsimd.indirect_dma_start(
                out=dst_tile, out_offset=None, in_=rows,
                in_offset=bass.IndirectOffsetOnAxis(ap=table, axis=0),
                bounds_check=bound, oob_is_err=False).then_inc(done, 16)

        @block.gpsimd
        def _(pool):
            last_row = pool.to_reg(EDGES_PAD - 1)
            nc.gpsimd.memset(msg[:, :, 0:HALF].bitcast(f32), 1.0).then_inc(cst_ready, 1)
            nc.gpsimd.memset(msg[:, :, HALF:ROW].bitcast(f32), 0.0).then_inc(cst_ready, 1)
            pool.wait_ge(ld_e, 32)

            def gather_edges(t0, turn_no, side):
                if not isinstance(turn_no, int) or turn_no >= 2:
                    for u in range(EU):
                        pool.wait_ge(got_dst[u], 16 * (turn_no - 1))
                nc.gpsimd.tensor_copy(src_now[:, side, :], srci[:, bass.ds(t0, EU)]).then_inc(idx_now, 1)
                nc.gpsimd.tensor_copy(dst_now[:, side, :], dsti[:, bass.ds(t0, EU)]).then_inc(idx_now, 1)
                pool.wait_ge(idx_now, 2 * turn_no + 2)
                for u in range(EU):
                    need_apart(pool, pool_passed, e_xt, t0 + (u - XE + 1))
                    gather(xsrc[:, u, :], src_now[:, side, u:u + 1], x, got_src[u])
                    gather(xdst[:, u, :], dst_now[:, side, u:u + 1], x, got_dst[u])

            E_TURNS = TILES // EU
            gather_edges(0, 0, 0)
            nc.gpsimd.memset(mg[:, :, :, :].bitcast(f32), 0.0).then_inc(node_ready, 1)
            nc.gpsimd.memset(halves[:, :], -0.5).then_inc(node_ready, 1)
            with pool.Fori(0, E_TURNS // 2) as g:
                for side in range(2):
                    gather_edges((g * 2 + (side + 1)) * EU, g * 2 + (side + 1), (side + 1) % 2)

            edges_done(pool)
            for u in range(EU):
                pool.wait_ge(e_stored[u], 16 * (TILES // EU))
            pool.wait_ge(tab_ready, 1)
            def node_stage(summed):
                def copy_rows(q, u):
                    need(pool, S["n_oh"], q - QU + 2)
                    nc.gpsimd.tensor_copy(rows_now[:, 2 * u:2 * u + 4], slot_row[:, bass.ds(2 * q, 4)])\
                        .then_inc(idx_now, 1)
                    pool.wait_ge(idx_now, 2 * E_TURNS + 1 + (q // 2 if isinstance(q, int) else (q - u) // 2 + u // 2))

                def gather_rows(q, u):
                    if u % 2 == 0 and not summed:
                        copy_rows(q, u)
                    for h in range(2):
                        to = mg[:, u, h, :].bitcast(f32)
                        need_apart(pool, pool_passed, S["n_seg"], q - QU + 1)
                        if summed:
                            nc.gpsimd.dma_start(to, sums[bass.ds((q * 2 + h) * P, P), :])\
                                .then_inc(got_m[2 * u + h], 16)
                        else:
                            gather(to, rows_now[:, 2 * u + h:2 * u + h + 1], messages, got_m[2 * u + h], last_row)

                def x_lo(q, u):
                    pool.wait_ge(S["n_xh"], q + 1)
                    need(pool, S["n_mm"], q - QU + 1)
                    nc.gpsimd.tensor_tensor(out=xl[:, u, :], in0=xts[:, u, :], in1=xh[:, u, :].bitcast(f32),
                                            op=ALU.subtract).then_inc(S["n_xl"], 1)

                def add_beta(q, u):
                    need(pool, S["n_u"], q - QU + 1)
                    pool.wait_ge(got_x[u], 16 * (uses(q, QU, u) + 1))
                    nc.gpsimd.tensor_tensor(out=xb[:, u, :], in0=xs[:, u, :], in1=betab[:, :], op=ALU.add)\
                        .then_inc(S["n_xb"], 1)

                def subtract_n(q, u):
                    need(pool, S["n_zd"], q - QU + 1)
                    pool.wait_ge(S["n_tanh"], q + 1)
                    nc.gpsimd.tensor_tensor(out=diff[:, u, :], in0=xs[:, u, :], in1=nt[:, u, :], op=ALU.subtract)\
                        .then_inc(S["n_diff"], 1)

                def inv_std(q, u, var, ve, free, rs, done):
                    pool.wait_ge(var, q + 1)
                    need(pool, free, q - QU + 1)
                    nc.gpsimd.tensor_tensor(out=rs[:, u, :], in0=ve[:, u, :], in1=halves[:, :], op=ALU.pow)\
                        .then_inc(done, 1)

                def inv_std1(q, u):
                    inv_std(q, u, S["n_v1"], ve1, S["n_u"], rs1, S["n_r1"])

                def inv_std2(q, u):
                    inv_std(q, u, S["n_v2"], ve2, S["n_y"], rs2, S["n_r2"])

                def s_lo(q, u):
                    pool.wait_ge(S["n_sh"], q + 1)
                    nc.gpsimd.tensor_tensor(out=sl[:, u % 2, :], in0=st[:, u % 2, :], in1=sh[:, u % 2, :].bitcast(f32),
                                            op=ALU.subtract).then_inc(S["n_sl"], 1)

                node_turns(pool, ((gather_rows, 4), (inv_std1, -3), (inv_std2, -4), (s_lo, 1), (x_lo, 2), (add_beta, -1),
                                  (subtract_n, -1)), first=-4, last=4)

            pool.wait_ge(ld_w, 16 * (W_LOADS))
            pool.wait_ge(lv_ready, 1)
            n_levels = pool.value_load(levels[0:1, 0:1], min_val=1, max_val=TILES)
            with pool.If(n_levels > 1):
                with pool.Fori(0, n_levels) as lv:
                    with pool.Fori(0, BLOCKS) as b:
                        n = lv * BLOCKS + b
                        pool.wait_ge(v_rows, lv + 1)
                        pool.wait_ge(v_sum, n + 1)
                        nc.gpsimd.tensor_copy(rows_now[:, 0:1], slot_row[:, bass.ds(b, 1)]).then_inc(v_idx, 1)
                        need_apart(pool, pool_passed, v_idx, n + 1)
                        gather(mg[:, 0, 0, :].bitcast(f32), rows_now[:, 0:1], messages, v_got, last_row)
                pool.wait_ge(v_done, 1)
                pool.wait_ge(tab_ready, 2)
                node_stage(True)
            with pool.Else():
                node_stage(False)

        @block.scalar
        def _(act):
            def edge_hi(t, u):
                act.wait_ge(e_xt, t + 1)
                need(act, e_mm, t - 1)
                nc.scalar.activation(eh[:, u % 2, :], pe_t[:, u % 2, :], ACT.Copy).then_inc(e_hi, 1)

            def edge_silu(t, u):
                act.wait_ge(e_mm, t + 1)
                need(act, e_ml, t - 1)
                nc.scalar.activation(sil[:, u % 2, :], pe_m[:, u % 2, 0:D], ACT.Silu).then_inc(e_msg, 1)
                act.wait_ge(e_msg, t + 1)
                nc.scalar.activation(pe_m[:, u % 2, 0:D], b1_all[:, :], ACT.Copy).then_inc(e_seed, 1)

            def edge_message_hi(t, u):
                act.wait_ge(e_msg, t + 1)
                need(act, e_stored[u], 16 * uses(t, EU, u))
                nc.scalar.activation(msg[:, u, 0:D], sil[:, u % 2, :], ACT.Copy).then_inc(e_mh, 1)

            act.wait_ge(ld_w1, 32)
            nc.scalar.activation(w1h[:, :, :], stage[:, :, :], ACT.Copy).then_inc(w1_hi, 1)
            act.wait_ge(b1_mm, 2)
            nc.scalar.activation(b1_all[:, :], pe_m[:, 0, 0:D], ACT.Copy).then_inc(b1_ready, 1)
            edge_hi(0, 0)
            act.wait_ge(cst_ready, 2)
            for t in range(EU):
                edge_hi(t + 1, (t + 1) % EU)
                edge_silu(t, t)
                edge_message_hi(t, t)
            with act.Fori(1, TILES // EU - 1) as g:
                for u in range(EU):
                    edge_hi(g * EU + (u + 1), (u + 1) % EU)
                    edge_silu(g * EU + u, u)
                    edge_message_hi(g * EU + u, u)
            for t in range(TILES - EU, TILES):
                if t + 1 < TILES:
                    edge_hi(t + 1, (t + 1) % EU)
                edge_silu(t, t % EU)
                edge_message_hi(t, t % EU)

            def gates0(q, u):
                act.wait_ge(S["n_g0"], q + 1)
                need(act, S["n_zd"], q - QU + 1)
                nc.scalar.activation(rz[:, u, 0, :], pn_rz[:, 0, :], ACT.Sigmoid).then_inc(S["n_rz0"], 1)

            def gates1(q, u):
                act.wait_ge(S["n_g1"], q + 1)
                nc.scalar.activation(rz[:, u, 1, :], pn_rz[:, 1, :], ACT.Sigmoid).then_inc(S["n_rz"], 1)

            def seed_n(q, u):
                act.wait_ge(S["n_si"], q + 1)
                nc.scalar.activation(pn_n[:, :, 0:D], hn_b[:, :, :], ACT.Copy).then_inc(S["n_sn"], 1)

            def x_hi(q, u):
                act.wait_ge(got_xt[u], 16 * (uses(q, QU, u) + 1))
                need(act, S["n_mm"], q - QU + 1)
                nc.scalar.activation(xh[:, u, :], xts[:, u, :], ACT.Copy).then_inc(S["n_xh"], 1)

            def mean_rows(q, u):
                act.wait_ge(S["n_rc"], q + 1)
                need(act, S["n_st"], q - 1)
                for h in range(2):
                    last = nc.scalar.activation(mean[:, u % 2, h, :], pn_s[:, h, 0:D], ACT.Copy,
                                                scale=rcount[:, u, h:h + 1])
                last.then_inc(S["n_mean"], 1)

            def s_hi(q, u):
                act.wait_ge(S["n_st"], q + 1)
                need(act, S["n_sl"], q - 1)
                nc.scalar.activation(st[:, u % 2, :], pn_t[:, u % 2, :], ACT.Copy)
                need(act, S["n_mm"], q - 1)
                nc.scalar.activation(sh[:, u % 2, :], pn_t[:, u % 2, :], ACT.Copy).then_inc(S["n_sh"], 1)

            def tanh(q, u):
                act.wait_ge(S["n_npre"], q + 1)
                need(act, S["n_xn"], q - QU + 1)
                nc.scalar.activation(nt[:, u, :], npre[:, u % 2, :], ACT.Tanh).then_inc(S["n_tanh"], 1)

            def last_norm(q, u):
                act.wait_ge(S["n_nmr"], q + 1)
                need(act, n_stored[u], 16 * uses(q, QU, u))
                for h in range(2):
                    last = nc.scalar.activation(yy[:, u, h * D:(h + 1) * D], uu[:, u, h * D:(h + 1) * D],
                                                ACT.Identity, bias=nmr[:, u, h:h + 1], scale=rs2[:, u, h:h + 1])
                last.then_inc(S["n_y"], 1)

            act.wait_ge(ld_w, 16 * W_LOADS)
            nc.scalar.activation(wxh[:, :, :], whh[:, :, :], ACT.Copy).then_inc(w_hi, 1)
            for k in range(KC):
                act.wait_ge(setup_mm, k + 1)
                for c, (n0, n1) in enumerate(((0, 2 * D), (2 * D, 3 * D))):
                    nc.scalar.activation(wsh[:, k, n0:n1], p_wc[k][:, c, 0:n1 - n0], ACT.Copy).then_inc(w_hi, 1)
            act.wait_ge(setup_mm, KC + 1)
            nc.scalar.activation(rz_b[:, :], p_rzb[:, 0, :], ACT.Copy).then_inc(w_hi, 1)
            nc.scalar.activation(rz_c[:, :], p_rzb[:, 1, :], ACT.Copy).then_inc(w_hi, 1)
            for h in range(2):
                nc.scalar.activation(hn_b[:, h, :], p_nb[:, 0, 0:D], ACT.Copy).then_inc(w_hi, 1)
            nc.scalar.activation(in_c[:, :], p_nb[:, 0, D:2 * D], ACT.Copy).then_inc(w_hi, 1)
            nc.scalar.activation(in_b[:, :], p_nb[:, 1, 0:D], ACT.Copy).then_inc(w_hi, 1)
            edges_done(act)
            act.wait_ge(primed, 1)
            node_turns(act, ((s_hi, 1), (x_hi, 2), (gates0, 0), (seed_n, 0), (tanh, -1), (mean_rows, 2), (gates1, 0),
                             (last_norm, -4)), first=-2, last=5)

        @block.vector
        def _(dve):
            dve.wait_ge(ld_e, 32)
            dve.wait_ge(ld_c, 16)
            steps = [
                lambda: nc.vector.tensor_copy(lower[:, :], cst[:, C_LOWER:C_LOWER + P]),
                lambda: nc.vector.tensor_copy(upto[:, :], cst[:, C_UPTO:C_UPTO + P]),
                lambda: nc.vector.tensor_copy(iota[:, :], cst[:, C_IOTA:C_IOTA + P]),
                lambda: nc.vector.tensor_copy(blocks[:, :], cst[:, C_BLOCK:C_BLOCK + BLOCKS]),
                lambda: nc.vector.tensor_scalar(iota1[:, :], cst[:, C_IOTA:C_IOTA + P], 1.0, None, ALU.add),
                lambda: nc.vector.tensor_scalar(pairi[:, :], srci[:, :], 8, None, ALU.arith_shift_right),
                lambda: nc.vector.tensor_scalar(parity[:, :], srci[:, :], 1, None, ALU.bitwise_and),
                lambda: nc.vector.tensor_scalar(place[:, :], srci[:, :], 1, None, ALU.arith_shift_right),
                lambda: nc.vector.memset(ones[:, :].bitcast(f32), 1.0),
            ]
            for f in steps:
                f().then_inc(idx_ready, 1)
            dve.wait_ge(idx_ready, len(steps))
            nc.vector.tensor_copy(pairf[:, :], pairi[:, :]).then_inc(idx_ready, 1)
            nc.vector.tensor_copy(parityf[:, :], parity[:, :]).then_inc(idx_ready, 1)
            nc.vector.tensor_scalar(loci[:, :], place[:, :], 127, None, ALU.bitwise_and).then_inc(idx_ready, 1)
            dve.wait_ge(idx_ready, len(steps) + 3)
            nc.vector.scalar_tensor_tensor(out=blkf[:, :], in0=pairf[:, :], scalar=2.0, in1=parityf[:, :],
                                           op0=ALU.mult, op1=ALU.add).then_inc(idx_ready, 1)
            nc.vector.tensor_scalar(locf[:, :], loci[:, :], 1.0, None, ALU.add).then_inc(idx_ready, 1)
            N_IDX = len(steps) + 5
            dve.wait_ge(w1_hi, 1)
            nc.vector.tensor_tensor(w1l[:, :, :], stage[:, :, :], w1h[:, :, :].bitcast(f32), ALU.subtract)\
                .then_inc(w_split, 1)

            dve.wait_ge(cst_ready, 2)
            dve.wait_ge(idx_ready, N_IDX)

            def edge_lo(t, u):
                dve.wait_ge(e_hi, t + 1)
                need(dve, e_mm, t - 1)
                nc.vector.tensor_tensor(el[:, u % 2, :], pe_t[:, u % 2, :], eh[:, u % 2, :].bitcast(f32),
                                        ALU.subtract).then_inc(e_lo, 1)

            def edge_block(t, u):
                need(dve, e_tab, t - 1)
                nc.vector.tensor_scalar(ohb[:, u % 2, :], blocks[:, :], blkf[:, bass.ds(t, 1)], None, ALU.is_equal)\
                    .then_inc(e_oh, 1)

            def edge_local(t, u):
                need(dve, e_stored[u], 16 * uses(t, EU, u))
                nc.vector.tensor_copy(msg[:, u, LOC:LOC + 1], locf[:, bass.ds(t, 1)]).then_inc(e_loc, 1)

            def edge_message_lo(t, u):
                dve.wait_ge(e_mh, t + 1)
                nc.vector.tensor_tensor(msg[:, u, HALF:HALF + D], sil[:, u % 2, :], msg[:, u, 0:D].bitcast(f32),
                                        ALU.subtract).then_inc(e_ml, 1)

            def edge_rank(t, u):
                dve.wait_ge(e_cum, t + 1)
                nc.vector.scalar_tensor_tensor(out=picked[:, :], in0=p_cum[:, 0:BLOCKS], scalar=1.0,
                                               in1=ohb[:, u % 2, :], op0=ALU.mult, op1=ALU.mult,
                                               accum_out=rank[:, u % 2:u % 2 + 1]).then_inc(e_rank, 1)

            def edge_slot(t, u):
                dve.wait_ge(e_rank, t + 1)
                need(dve, e_tab, t - 1)
                r = rank[:, u % 2:u % 2 + 1]
                nc.vector.tensor_scalar(oha[:, u % 2, :], iota[:, :], r, cst[:, bass.ds(C_CODE + t, 1)],
                                        ALU.is_equal, ALU.mult).then_inc(e_one, 1)
                nc.vector.tensor_copy(ranks[:, bass.ds(t, 1)], r).then_inc(e_one, 1)

            edge_lo(0, 0)
            edge_block(0, 0)

            def edge_turn(t0, more=True):
                for u in range(EU):
                    t = t0 + u
                    edge_rank(t, u)
                    if not isinstance(t0, int) or t > 0:
                        edge_message_lo(t0 + (u - 1), (u - 1) % EU)
                    if more or u + 1 < EU:
                        edge_block(t0 + (u + 1), (u + 1) % EU)
                    edge_slot(t, u)
                    if more or u + 1 < EU:
                        edge_lo(t0 + (u + 1), (u + 1) % EU)
                    edge_local(t, u)

            edge_turn(0)
            with dve.Fori(1, TILES // EU - 1) as g:
                edge_turn(g * EU)
            edge_turn(TILES - EU, more=False)
            edge_message_lo(TILES - 1, (TILES - 1) % EU)

            def make_table(step, n, done):
                code = p_tab[:, 0:BLOCKS].bitcast(i32)
                high, low, place_ = (slot_bits[:, k, :] for k in range(3))
                empty, first, row, summed = (slot_parts[:, k, :] for k in range(4))
                nc.vector.tensor_scalar(slot_used[:, :], p_tab[:, 0:BLOCKS], 0.0, None, ALU.is_gt).then_inc(step, 1)
                nc.vector.tensor_scalar(empty, p_tab[:, 0:BLOCKS], 0.0, EMPTY, ALU.is_equal, ALU.mult).then_inc(step, 1)
                nc.vector.tensor_scalar(high, code, 23, None, ALU.arith_shift_right).then_inc(step, 1)
                nc.vector.tensor_scalar(low, code, 13, T_LOW - 1, ALU.arith_shift_right, ALU.bitwise_and)\
                    .then_inc(step, 1)
                nc.vector.tensor_scalar(place_, code, 16, P - 1, ALU.arith_shift_right, ALU.bitwise_and)\
                    .then_inc(step, 1)
                dve.wait_ge(step, n + 5)
                nc.vector.tensor_scalar(first, high, float(-CODE_EXP), float(T_LOW * P), ALU.add, ALU.mult)\
                    .then_inc(step, 1)
                nc.vector.scalar_tensor_tensor(out=row, in0=low, scalar=float(P), in1=place_,
                                               op0=ALU.mult, op1=ALU.add).then_inc(step, 1)
                dve.wait_ge(step, n + 7)
                nc.vector.tensor_tensor(summed, first, row, ALU.add).then_inc(step, 1)
                dve.wait_ge(step, n + 8)
                nc.vector.tensor_tensor(slot_row[:, :], summed, empty, ALU.add).then_inc(done, 1)

            TABLE_STEPS = 8
            dve.wait_ge(ld_w, 16 * W_LOADS)
            for k in range(KC):
                nc.vector.tensor_scalar(b2b[:, k, :], ones[:, :].bitcast(f32), b2s[:, k:k + 1], None, ALU.mult)\
                    .then_inc(b2_ready, 1)
            dve.wait_ge(e_one, 2 * TILES)
            nc.vector.reduce_max(top[:, :], ranks[:, :], axis=mybir.AxisListType.X).then_inc(lv_top, 1)
            dve.wait_ge(e_tab, TILES)
            make_table(t_step, 0, tab_ready)
            dve.wait_ge(lv_row, 1)
            nc.vector.reduce_max(levf[:, :], p_cum[0:1, 0:P], axis=mybir.AxisListType.X).then_inc(lv_top, 1)
            dve.wait_ge(lv_top, 2)
            nc.vector.tensor_scalar(levi[:, :], levf[:, :], float(P), None, ALU.add).then_inc(lv_top, 1)
            dve.wait_ge(lv_top, 3)
            nc.vector.tensor_scalar(levels[:, :], levi[:, :], 7, None, ALU.arith_shift_right).then_inc(lv_ready, 1)

            dve.wait_ge(w_hi, 1)
            nc.vector.tensor_tensor(wxl[:, :, :], whh[:, :, :], wxh[:, :, :].bitcast(f32), ALU.subtract)\
                .then_inc(setup_cp, 1)
            for k in range(KC):
                for c, (n0, n1) in enumerate(((0, 2 * D), (2 * D, 3 * D))):
                    dve.wait_ge(w_hi, 2 + 2 * k + c)
                    nc.vector.tensor_tensor(wsl[:, k, n0:n1], p_wc[k][:, c, 0:n1 - n0], wsh[:, k, n0:n1].bitcast(f32),
                                            ALU.subtract).then_inc(setup_cp, 1)
            dve.wait_ge(lv_ready, 1)
            n_levels = dve.value_load(levels[0:1, 0:1], min_val=1, max_val=TILES)
            with dve.If(n_levels > 1):
                nc.vector.memset(put[:, :].bitcast(f32), 0.0).then_inc(v_zero, 1)
                dve.wait_ge(v_zero, 1)
                nc.vector.tensor_copy(put[:, LOC:LOC + 1], cst[:, C_PART:C_PART + 1]).then_inc(v_zero, 1)
                with dve.Fori(0, n_levels) as lv:
                    with dve.Fori(0, TILES) as t:
                        dve.wait_ge(v_tab, lv * TILES + t + 1)
                        nc.vector.tensor_scalar(ohb[:, 0, :], blocks[:, :], blkf[:, bass.ds(t, 1)], None,
                                                ALU.is_equal).then_inc(v_oh, 1)
                        nc.vector.tensor_scalar(oha[:, 0, :], iota[:, :], ranks[:, bass.ds(t, 1)],
                                                cst[:, bass.ds(C_CODE + t, 1)], ALU.is_equal, ALU.mult)\
                            .then_inc(v_oh, 1)
                    dve.wait_ge(v_tab, lv * TILES + TILES + 1)
                    make_table(v_step, lv * (TABLE_STEPS + 1), v_rows)
                    nc.vector.tensor_scalar(ranks[:, :], ranks[:, :], float(-P), None, ALU.add).then_inc(v_step, 1)
                    need_apart(dve, dve_passed, v_step, (lv + 1) * (TABLE_STEPS + 1))
                    with dve.Fori(0, BLOCKS) as b:
                        n = lv * BLOCKS + b
                        dve.wait_ge(v_got, n * 16 + 16)
                        nc.vector.tensor_scalar(oh[:, 0, 0, :], iota1[:, :], mg[:, 0, 0, LOC:LOC + 1].bitcast(f32),
                                                slot_used[:, bass.ds(b, 1)], ALU.is_equal, ALU.mult)\
                            .then_inc(v_one, 1)
                        dve.wait_ge(v_sum, n + 2)
                        dve.wait_ge(v_prev, n * 16 + 16)
                        nc.vector.tensor_tensor(total[:, 0, :], pn_s[:, 0, 0:SUMMED],
                                                before[:, 0:SUMMED].bitcast(f32), ALU.add).then_inc(v_acc, 1)
                        dve.wait_ge(v_acc, n * 3 + 1)
                        nc.vector.tensor_tensor(total[:, 1, :], total[:, 0, :],
                                                before[:, HALF:HALF + SUMMED].bitcast(f32), ALU.add)\
                            .then_inc(v_acc, 1)
                        dve.wait_ge(v_acc, n * 3 + 2)
                        nc.vector.tensor_copy(put[:, 0:SUMMED], total[:, 1, :]).then_inc(v_acc, 1)
                        dve.wait_ge(v_acc, n * 3 + 3)
                        nc.vector.tensor_tensor(put[:, HALF:HALF + SUMMED], total[:, 1, :],
                                                put[:, 0:SUMMED].bitcast(f32), ALU.subtract).then_inc(v_add, 1)
                nc.vector.memset(slot_used[:, :], 1.0).then_inc(tab_ready, 1)
                dve.wait_ge(tab_ready, 2)

            def one_hot(q, u):
                need(dve, S["n_seg"], q - QU + 1)
                for h in range(2):
                    dve.wait_ge(got_m[2 * u + h], 16 * (uses(q, QU, u) + 1))
                    last = nc.vector.tensor_scalar(oh[:, u, h, :], iota1[:, :],
                                                   mg[:, u, h, LOC:LOC + 1].bitcast(f32),
                                                   slot_used[:, bass.ds(q * 2 + h, 1)], ALU.is_equal, ALU.mult)
                last.then_inc(S["n_oh"], 1)

            def gated_h(q, u):
                dve.wait_ge(S["n_rz"], q + 1)
                dve.wait_ge(S["n_mm"], q + 1)
                nc.vector.tensor_tensor(rhn[:, u % 2, :, :], rz[:, u, :, 0:D], pn_n[:, :, 0:D], ALU.mult)\
                    .then_inc(S["n_rhn"], 1)

            def n_input(q, u):
                dve.wait_ge(S["n_rhn"], q + 1)
                need(dve, S["n_tanh"], q - 1)
                nc.vector.tensor_tensor(npre[:, u % 2, :].rearrange("p (h d) -> p h d", h=2), rhn[:, u % 2, :, :],
                                        pn_n[:, :, D:2 * D], ALU.add).then_inc(S["n_npre"], 1)

            def count_eps(q, u):
                dve.wait_ge(S["n_seg"], q + 1)
                nc.vector.tensor_scalar(cnt_eps[:, u, :], pn_s[:, :, CNT], EPS_CNT, None, ALU.add)\
                    .then_inc(S["n_ce"], 1)

            def has_edges(q, u):
                dve.wait_ge(S["n_seg"], q + 1)
                need(dve, S["n_sn"], q - QU + 1)
                nc.vector.tensor_scalar(has[:, u, :], pn_s[:, :, CNT], 1.0, None, ALU.min).then_inc(S["n_has"], 1)

            def seed_rz(q, u, h, free, done):
                dve.wait_ge(S["n_has"], q + 1)
                need(dve, S[free], q)
                nc.vector.scalar_tensor_tensor(out=pn_rz[:, h, :], in0=rz_c[:, :], scalar=has[:, u, h:h + 1],
                                               in1=rz_b[:, :], op0=ALU.mult, op1=ALU.add).then_inc(S[done], 1)

            def seed_i(q, u):
                dve.wait_ge(S["n_has"], q + 1)
                need(dve, S["n_npre"], q)
                for h in range(2):
                    last = nc.vector.scalar_tensor_tensor(out=pn_n[:, h, D:2 * D], in0=in_c[:, :],
                                                          scalar=has[:, u, h:h + 1], in1=in_b[:, :],
                                                          op0=ALU.mult, op1=ALU.add)
                last.then_inc(S["n_si"], 1)

            def seed_rz0(q, u):
                seed_rz(q, u, 0, "n_rz0", "n_sd0")

            def seed_rz1(q, u):
                seed_rz(q, u, 1, "n_rz", "n_sd1")

            def count_inv(q, u):
                dve.wait_ge(S["n_ce"], q + 1)
                need(dve, S["n_mean"], q - QU + 1)
                nc.vector.reciprocal(rcount[:, u, :], cnt_eps[:, u, :]).then_inc(S["n_rc"], 1)

            def z_diff(q, u):
                dve.wait_ge(S["n_diff"], q + 1)
                nc.vector.tensor_tensor(zd[:, u % 2, :].rearrange("p (h d) -> p h d", h=2), rz[:, u, :, D:2 * D],
                                        diff[:, u, :].rearrange("p (h d) -> p h d", h=2), ALU.mult)\
                    .then_inc(S["n_zd"], 1)

            def x_new(q, u):
                dve.wait_ge(S["n_zd"], q + 1)
                nc.vector.tensor_tensor(xn[:, u % 2, :], zd[:, u % 2, :], nt[:, u, :], ALU.add)\
                    .then_inc(S["n_xn"], 1)

            def stats(q, u, tile, before, st, done):
                dve.wait_ge(before, q + 1)
                for h in range(2):
                    last = nc.vector.bn_stats(st[:, u, h, :], tile[:, h * D:(h + 1) * D])
                last.then_inc(done, 1)

            def aggregate(q, u, before, st, ag, done):
                need_apart(dve, dve_passed, before, q + 1)
                for h in range(2):
                    last = nc.vector.bn_aggr(ag[:, u, h, :], st[:, u, h, :])
                last.then_inc(done, 1)

            def var_eps(q, u, before, ag, ve, done):
                dve.wait_ge(before, q + 1)
                nc.vector.tensor_scalar(ve[:, u, :], ag[:, u, :, 1], EPS_LN, None, ALU.add).then_inc(done, 1)

            def scale_gamma(q, u):
                dve.wait_ge(S["n_a1"], q + 1)
                for h in range(2):
                    last = nc.vector.scalar_tensor_tensor(
                        out=tg[:, u % 2, h * D:(h + 1) * D], in0=xn[:, u % 2, h * D:(h + 1) * D],
                        scalar=ag1[:, u, h, 0:1], in1=gammab[:, :], op0=ALU.subtract, op1=ALU.mult)
                last.then_inc(S["n_tg"], 1)

            def residual(q, u):
                dve.wait_ge(S["n_tg"], q + 1)
                dve.wait_ge(S["n_r1"], q + 1)
                dve.wait_ge(S["n_xb"], q + 1)
                need(dve, S["n_y"], q - QU + 1)
                for h in range(2):
                    last = nc.vector.scalar_tensor_tensor(
                        out=uu[:, u, h * D:(h + 1) * D], in0=tg[:, u % 2, h * D:(h + 1) * D],
                        scalar=rs1[:, u, h:h + 1], in1=xb[:, u, h * D:(h + 1) * D], op0=ALU.mult, op1=ALU.add)
                last.then_inc(S["n_u"], 1)

            def minus_mean(q, u):
                dve.wait_ge(S["n_r2"], q + 1)
                nc.vector.scalar_tensor_tensor(out=nmr[:, u, :], in0=ag2[:, u, :, 0], scalar=-1.0, in1=rs2[:, u, :],
                                               op0=ALU.mult, op1=ALU.mult).then_inc(S["n_nmr"], 1)

            def stats1(q, u):
                stats(q, u, xn[:, u % 2, :], S["n_xn"], st1, S["n_s1"])

            def stats2(q, u):
                stats(q, u, uu[:, u, :], S["n_u"], st2, S["n_s2"])

            def aggregate1(q, u):
                aggregate(q, u, S["n_s1"], st1, ag1, S["n_a1"])

            def aggregate2(q, u):
                aggregate(q, u, S["n_s2"], st2, ag2, S["n_a2"])

            def var_eps1(q, u):
                var_eps(q, u, S["n_a1"], ag1, ve1, S["n_v1"])

            def var_eps2(q, u):
                var_eps(q, u, S["n_a2"], ag2, ve2, S["n_v2"])

            edges_done(dve)
            dve.wait_ge(primed, 1)
            dve.wait_ge(w_hi, 2 * KC + 7)
            node_turns(dve, ((gated_h, -1), (z_diff, -2), (n_input, -1), (count_eps, 2), (has_edges, 2), (seed_i, 0), (x_new, -2),
                             (count_inv, 2), (minus_mean, -4), (seed_rz0, 1), (residual, -3), (stats1, -2),
                             (stats2, -3), (aggregate1, -2), (one_hot, 3), (aggregate2, -3), (var_eps1, -2),
                             (seed_rz1, 1), (var_eps2, -3), (scale_gamma, -2)), first=-3, last=4)

        @block.tensor
        def _(pe):
            def mm(out_, lhsT, rhs, start, stop, skip=False):
                return nc.tensor.matmul(out_, lhsT, rhs, start=start, stop=stop, skip_group_check=skip)

            pe.wait_ge(ld_c, 16)
            pe.wait_ge(idx_ready, 9)
            pe.wait_ge(ld_w1, 32)
            for k in range(2):
                mm(pe_m[:, k, 0:D], ones[0:1, :].bitcast(f32), brow[:, 6 * D:7 * D], True, True).then_inc(b1_mm, 1)

            def edge_transpose(t, u):
                pe.wait_ge(got_src[u], 16 * (uses(t, EU, u) + 1))
                pe.wait_ge(got_dst[u], 16 * (uses(t, EU, u) + 1))
                need(pe, e_lo, t - 1)
                for c in range(2 * KC):
                    tile = (xsrc if c < KC else xdst)[:, u, (c % KC) * P:(c % KC + 1) * P]
                    last = nc.tensor.transpose(pe_t[:, u % 2, c * P:(c + 1) * P], tile, ident)
                last.then_inc(e_xt, 1)

            def edge_earlier(t, u, first=False):
                pe.wait_ge(e_oh, t + 1)
                mm(p_cum[:, 0:BLOCKS], lower[:, :], ohb[:, u % 2, :], first, True, True).then_inc(e_cum, 1)

            def edge_products(t, u):
                pe.wait_ge(e_lo, t + 1)
                need(pe, e_seed, t - 1)
                o = pe_m[:, u % 2, 0:D]
                for c in range(2 * KC):
                    h, l = (a[:, u % 2, c * P:(c + 1) * P] for a in (eh, el))
                    mm(o, h, w1h[:, c, :], False, False, True)
                    mm(o, h, w1l[:, c, :], False, False, True)
                    last = mm(o, l, w1h[:, c, :], False, True, True)
                last.then_inc(e_mm, 1)

            def edge_table(t, u, first=False):
                pe.wait_ge(e_rank, t + 1)
                mm(p_cum[:, 0:BLOCKS], upto[:, :], ohb[:, u % 2, :], False, True, True)
                pe.wait_ge(e_one, 2 * t + 1)
                mm(p_tab[:, 0:BLOCKS], oha[:, u % 2, :], ohb[:, u % 2, :], first, True, True).then_inc(e_tab, 1)

            edge_transpose(0, 0)
            pe.wait_ge(w_split, 1)
            pe.wait_ge(b1_ready, 1)

            def edge_turn(t0, more=True, first=False):
                for u in range(EU):
                    t = t0 + u
                    edge_earlier(t, u, first and u == 0)
                    if more or u + 1 < EU:
                        edge_transpose(t0 + (u + 1), (u + 1) % EU)
                    edge_products(t, u)
                    edge_table(t, u, first and u == 0)

            edge_turn(0, first=True)
            with pe.Fori(1, TILES // EU - 1) as g:
                edge_turn(g * EU)
            edge_turn(TILES - EU, more=False)

            def segment_products(bank, one_hots, rows):
                mm(bank[:, 0:SUMMED], one_hots, rows[:, 0:SUMMED], True, False)
                return mm(bank[:, 0:SUMMED], one_hots, rows[:, HALF:HALF + SUMMED], False, True)

            pe.wait_ge(lv_top, 1)
            mm(p_cum[0:1, 0:P], top[:, :], ident, True, True).then_inc(lv_row, 1)

            pe.wait_ge(ld_w, 16 * W_LOADS)
            pe.wait_ge(e_seed, TILES)
            pe.wait_ge(e_lo, TILES)
            for i in range(KC):
                for c, (n0, n1) in enumerate(((0, 2 * D), (2 * D, 3 * D))):
                    for o in range(KC):
                        last = mm(p_wc[i][:, c, 0:n1 - n0], w2s[:, o, i * P:(i + 1) * P], wih[:, o, n0:n1],
                                  o == 0, o == KC - 1)
                last.then_inc(setup_mm, 1)
            one = ones[0:1, :].bitcast(f32)
            pe.wait_ge(b2_ready, KC)
            pe.wait_ge(tab_ready, 1)
            pe.wait_ge(lv_top, 2)
            mm(p_rzb[:, 0, :], one, brow[:, 0:2 * D], True, False)
            mm(p_rzb[:, 0, :], one, brow[:, 3 * D:5 * D], False, True)
            mm(p_nb[:, 0, 0:D], one, brow[:, 5 * D:6 * D], True, True)
            for o in range(KC):
                mm(p_rzb[:, 1, :], b2b[:, o, :], wih[:, o, 0:2 * D], o == 0, o == KC - 1)
            for o in range(KC):
                mm(p_nb[:, 0, D:2 * D], b2b[:, o, :], wih[:, o, 2 * D:3 * D], o == 0, o == KC - 1)
            mm(p_nb[:, 1, 0:D], one, brow[:, 2 * D:3 * D], True, True).then_inc(setup_mm, 1)
            pe.wait_ge(w_hi, 2 * KC + 7)
            pe.wait_ge(setup_cp, WC_PARTS)

            pe.wait_ge(lv_ready, 1)
            n_levels = pe.value_load(levels[0:1, 0:1], min_val=1, max_val=TILES)
            with pe.If(n_levels > 1):
                pe.sem_inc(v_tab)
                pe.sem_inc(v_sum)
                with pe.Fori(0, n_levels) as lv:
                    def level_tile(t, first):
                        pe.wait_ge(v_oh, (lv * TILES + t) * 2 + 2)
                        mm(p_tab[:, 0:BLOCKS], oha[:, 0, :], ohb[:, 0, :], first, True, True).then_inc(v_tab, 1)
                    level_tile(0, True)
                    with pe.Fori(1, TILES) as t:
                        level_tile(t, False)
                    with pe.Fori(0, BLOCKS) as b:
                        pe.wait_ge(v_one, lv * BLOCKS + b + 1)
                        segment_products(pn_s[:, 0, :], oh[:, 0, 0, :], mg[:, 0, 0, :]).then_inc(v_sum, 1)

            def segment_sum(q, u):
                pe.wait_ge(S["n_oh"], q + 1)
                need(pe, S["n_mean"], q)
                for h in range(2):
                    one_hots, rows = oh[:, u, h, :], mg[:, u, h, :]
                    last = segment_products(pn_s[:, h, :], one_hots, rows)
                last.then_inc(S["n_seg"], 1)

            def s_transpose(q, u):
                pe.wait_ge(S["n_mean"], q + 1)
                need(pe, S["n_sh"], q - 1)
                for h in range(2):
                    for c in range(KC):
                        last = nc.tensor.transpose(pn_t[:, u % 2, (2 * h + c) * P:(2 * h + c + 1) * P],
                                                   mean[:, u % 2, h, c * P:(c + 1) * P], ident)
                last.then_inc(S["n_st"], 1)

            def products(q, u):
                pe.wait_ge(S["n_xl"], q + 1)
                pe.wait_ge(S["n_sl"], q + 1)

                def part(o, side, h, n0, n1):
                    hi, lo, whi, wlo = side
                    for c in range(KC):
                        a, b = (t[:, (2 * h + c) * P:(2 * h + c + 1) * P] for t in (hi, lo))
                        mm(o, a, whi[:, c, n0:n1], False, False, True)
                        mm(o, a, wlo[:, c, n0:n1], False, False, True)
                        last = mm(o, b, whi[:, c, n0:n1], False, True, True)
                    return last

                x_ = xh[:, u, :], xl[:, u, :], wxh, wxl
                s_ = sh[:, u % 2, :], sl[:, u % 2, :], wsh, wsl
                for h in range(2):
                    pe.wait_ge(S[f"n_sd{h}"], q + 1)
                    part(pn_rz[:, h, :], x_, h, 0, 2 * D)
                    part(pn_rz[:, h, :], s_, h, 0, 2 * D).then_inc(S[f"n_g{h}"], 1)
                pe.wait_ge(S["n_sn"], q + 1)
                for h in range(2):
                    part(pn_n[:, h, 0:D], x_, h, 2 * D, 3 * D)
                    last = part(pn_n[:, h, D:2 * D], s_, h, 2 * D, 3 * D)
                last.then_inc(S["n_mm"], 1)

            for banks in (pn_rz, pn_n):
                for h in range(2):
                    last = mm(banks[:, h, :], ones[:, :], wxh[:, 0, 0:2 * D], True, True)
            last.then_inc(primed, 1)
            node_turns(pe, ((s_transpose, 1), (segment_sum, 2), (products, 0)), first=-2, last=0)


def kernel(x, src, dst, L0_gnn_W1, L0_gnn_b1, L0_gnn_W2, L0_gnn_b2, L0_gnn_w_ih, L0_gnn_w_hh,
           L0_gnn_b_ih, L0_gnn_b_hh, L0_gnn_gamma, L0_gnn_beta):
    import concourse.bacc as bacc
    from concourse.bass_utils import run_bass_kernel_spmd

    def arr(a):
        return np.ascontiguousarray(np.asarray(a))
    x, src, dst = arr(x), arr(src), arr(dst)
    xp = np.zeros((NODES_PAD, D), x.dtype)
    xp[:NODES] = x
    pad = EDGES_PAD - EDGES
    srcp = np.concatenate([src, (NODES_PAD - 1 - 2 * np.arange(pad)).astype(src.dtype)])
    xt = xp.reshape(PAIRS, P, 2, KC, P).transpose(0, 4, 2, 3, 1).reshape(PAIRS * P, 2 * D)
    dstp = np.concatenate([dst, np.zeros(pad, dst.dtype)])
    ins = {
        "x": xp, "xt": arr(xt), "src": srcp, "dst": dstp, "w1t": arr(arr(L0_gnn_W1).T), "b1": arr(L0_gnn_b1),
        "w2": arr(L0_gnn_W2), "b2": arr(L0_gnn_b2), "wiht": arr(arr(L0_gnn_w_ih).T),
        "whht": arr(arr(L0_gnn_w_hh).T), "bih": arr(L0_gnn_b_ih), "bhh": arr(L0_gnn_b_hh),
        "gamma": arr(L0_gnn_gamma), "beta": arr(L0_gnn_beta), "consts": constants(),
    }
    nc = bacc.Bacc("TRN2", target_bir_lowering=False, num_devices=1)
    arrays, args = {}, []
    for name, a in ins.items():
        arrays[f"in_{name}"] = a
        args.append(nc.dram_tensor(f"in_{name}", a.shape, mybir.dt.from_np(a.dtype), kind="ExternalInput").ap())
    args.append(nc.dram_tensor("out_y", (NODES_PAD, D), mybir.dt.float32, kind="ExternalOutput").ap())
    gnn_layer(nc, *args)
    r = run_bass_kernel_spmd(nc, [arrays], core_ids=[0])
    return r.results[0]["out_y"][:NODES]
```
